# Optimizing a Trainium2 kernel written in Bass

```python
import numpy as np
import jax
import jax.numpy as jnp

def _softmax(x, axis=-1):
    return jax.nn.softmax(x, axis=axis)

def _gelu(x):
    return jax.nn.gelu(x, approximate=True)

def _silu(x):
    return jax.nn.silu(x)

def _sigmoid(x):
    return jax.nn.sigmoid(x)

def _layernorm(x, axis=-1, eps=1e-05):
    m = jnp.mean(x, axis=axis, keepdims=True)
    v = jnp.var(x, axis=axis, keepdims=True)
    return (x - m) / jnp.sqrt(v + eps)

def _scatter_add(tgt, idx, src, axis=0):
    return tgt.at[idx].add(src)

def _segment_sum(src, seg, n):
    return jax.ops.segment_sum(src, seg, n)
kernel_name = 'mk_adj_resnorm_d2_adj_r2_c6b4b3'

def setup_inputs(seed: int=0):
    np.random.seed(seed)
    _w = jnp.asarray

    def _rec_inputs():
        import jax
        import jax.numpy as jnp
        _gk = jax.random.key(seed)
        x = 0.0001732 + 1 * jax.random.normal(jax.random.fold_in(_gk, 1), (5120, 64), jnp.float32)
        _a = jax.random.bernoulli(jax.random.fold_in(_gk, 2), 0.0015625, (5120, 5120))
        _af = _a.astype(jnp.float32)
        _af = _af * jax.random.uniform(jax.random.fold_in(_gk, 3), (5120, 5120), jnp.float32, 0.05, 0.02)
        adj = _af
        return (x, adj)
    x, adj = _rec_inputs()

    def _L0_gnn_setup():
        import jax, jax.numpy as jnp
        import numpy as np
        N_USERS = 2048
        N_ITEMS = 3072
        EMB = 64
        LN_EPS = 1e-05
        key = jax.random.key(seed)
        ks = jax.random.split(key, 10)
        N = N_USERS + N_ITEMS
        ego = jax.random.normal(ks[0], (N, EMB), jnp.float32)
        adj = (jax.random.uniform(ks[1], (N, N), jnp.float32) < 0.01).astype(jnp.float32) * 0.02
        xav = float(np.sqrt(6.0 / (EMB + EMB)))
        W_u = jax.random.uniform(ks[2], (EMB, EMB), jnp.float32, -xav, xav)
        W_i = jax.random.uniform(ks[3], (EMB, EMB), jnp.float32, -xav, xav)
        diag_u = jax.random.uniform(ks[4], (N_USERS,), jnp.float32, 0.99, 1.01)
        diag_i = jax.random.uniform(ks[5], (N_ITEMS,), jnp.float32, 0.99, 1.01)
        par_u = jax.random.uniform(ks[6], (2,), jnp.float32, 0.0, 0.99)
        par_i = jax.random.uniform(ks[7], (2,), jnp.float32, 0.0, 0.99)
        ln_gamma = jnp.ones((EMB,), jnp.float32)
        ln_beta = jnp.zeros((EMB,), jnp.float32)
        return {'ego_embeddings': ego, 'adj': adj, 'W_u': W_u, 'diag_u': diag_u, 'par_u': par_u, 'W_i': W_i, 'diag_i': diag_i, 'par_i': par_i, 'ln_gamma': ln_gamma, 'ln_beta': ln_beta}
    _L0_gnn_all = _L0_gnn_setup()
    _L0_gnn_in = {k: v for k, v in _L0_gnn_all.items() if k in ('W_u', 'diag_u', 'par_u', 'W_i', 'diag_i', 'par_i', 'ln_gamma', 'ln_beta')}
    del _L0_gnn_all

    def _L1_gnn_setup():
        import jax, jax.numpy as jnp
        import numpy as np
        N, D_IN, D_OUT = (4096, 64, 64)
        MAX_NEIGH = 100
        DECAY = 0.5
        key = jax.random.key(seed)
        k1, k2, k3, k4 = jax.random.split(key, 4)
        stdv = 1.0 / np.sqrt(D_OUT)
        inputs = {'input': jax.random.normal(k1, (N, D_IN), dtype=jnp.float32), 'adj': jax.random.randint(k2, (N, N), 0, 2).astype(jnp.float32), 'weight': jax.random.uniform(k3, (D_IN, D_OUT), minval=-stdv, maxval=stdv, dtype=jnp.float32), 'bias': jax.random.uniform(k4, (D_OUT,), minval=-stdv, maxval=stdv, dtype=jnp.float32)}
        return inputs
    _L1_gnn_all = _L1_gnn_setup()
    _L1_gnn_in = {k: v for k, v in _L1_gnn_all.items() if k in ('weight', 'bias')}
    del _L1_gnn_all
    return {'x': x, 'adj': adj, 'L0_gnn_W_u': _L0_gnn_in['W_u'], 'L0_gnn_diag_u': _L0_gnn_in['diag_u'], 'L0_gnn_par_u': _L0_gnn_in['par_u'], 'L0_gnn_W_i': _L0_gnn_in['W_i'], 'L0_gnn_diag_i': _L0_gnn_in['diag_i'], 'L0_gnn_par_i': _L0_gnn_in['par_i'], 'L0_gnn_ln_gamma': _L0_gnn_in['ln_gamma'], 'L0_gnn_ln_beta': _L0_gnn_in['ln_beta'], 'L1_gnn_weight': _L1_gnn_in['weight'], 'L1_gnn_bias': _L1_gnn_in['bias']}

def reference(x, adj, L0_gnn_W_u, L0_gnn_diag_u, L0_gnn_par_u, L0_gnn_W_i, L0_gnn_diag_i, L0_gnn_par_i, L0_gnn_ln_gamma, L0_gnn_ln_beta, L1_gnn_weight, L1_gnn_bias):
    import jax
    import jax.numpy as jnp

    def _L0_gnn_ref(ego_embeddings, adj, W_u, diag_u, par_u, W_i, diag_i, par_i, ln_gamma, ln_beta):
        import jax, jax.numpy as jnp
        import numpy as np
        N_USERS = 2048
        N_ITEMS = 3072
        EMB = 64
        LN_EPS = 1e-05
        nu = diag_u.shape[0]
        res = ego_embeddings
        ego_u = ego_embeddings[:nu]
        ego_i = ego_embeddings[nu:]
        u = par_u[0] * par_u[1] * (diag_u[:, None] * ego_u @ W_u) + ego_u
        i = par_i[0] * par_i[1] * (diag_i[:, None] * ego_i @ W_i) + ego_i
        e = jnp.concatenate([u, i], axis=0)
        h = adj @ (adj.T @ e)
        mu = jnp.mean(h, axis=-1, keepdims=True)
        var = jnp.var(h, axis=-1, keepdims=True)
        out = (h - mu) * jax.lax.rsqrt(var + LN_EPS) * ln_gamma + ln_beta + res
        return out

    def _L1_gnn_ref(input, adj, weight, bias):
        import jax, jax.numpy as jnp
        import numpy as np
        N, D_IN, D_OUT = (4096, 64, 64)
        MAX_NEIGH = 100
        DECAY = 0.5
        support = input @ weight
        mask = (adj != 0).astype(support.dtype)
        rank = jnp.cumsum(mask, axis=1)
        deg = rank[:, -1:]
        k = jnp.minimum(deg, float(MAX_NEIGH))
        pos = rank - (deg - k)
        w = mask * jnp.where(pos > 0, DECAY ** (k - pos), 0.0)
        out = w @ support + bias
        return out
    x = _layernorm(x + _L0_gnn_ref(x, adj, L0_gnn_W_u, L0_gnn_diag_u, L0_gnn_par_u, L0_gnn_W_i, L0_gnn_diag_i, L0_gnn_par_i, L0_gnn_ln_gamma, L0_gnn_ln_beta), axis=-1)
    x = _layernorm(x + _L1_gnn_ref(x, adj, L1_gnn_weight, L1_gnn_bias), axis=-1)
    return x

_drawn_inputs = setup_inputs


def setup_inputs(seed=0):
    import zlib

    import numpy as np

    out = dict(_drawn_inputs(seed))
    spreads = {'L0_gnn_ln_gamma': (1.0, 0.2), 'L0_gnn_ln_beta': (0.0, 0.1)}
    factors = {'L0_gnn_diag_u': 8.0, 'L0_gnn_W_i': 5.84, 'L0_gnn_diag_i': 8.0}
    for name, (base, spread) in spreads.items():
        noise = np.random.default_rng([zlib.crc32(name.encode()), seed]).standard_normal(out[name].shape)
        drawn = base * np.exp(spread * noise) if base else spread * noise
        out[name] = jnp.asarray(drawn.astype(out[name].dtype))
    for name, factor in factors.items():
        out[name] = (out[name] * factor).astype(out[name].dtype)
    return out
```

```python
from contextlib import ExitStack

import concourse.bass as bass
from concourse import mybir

F32 = mybir.dt.float32
BF16 = mybir.dt.bfloat16
U8 = mybir.dt.uint8
U16 = mybir.dt.uint16
ALU = mybir.AluOpType
ACT = mybir.ActivationFunctionType
AX = mybir.AxisListType.X

P = 128
N = 5120
D = 64
N_USERS = 2048
MAX_NEIGH = 100
LN_EPS = 1e-5
BLOCKS = N // P
CHUNK = 512
CHUNKS = N // CHUNK
PER_CHUNK = CHUNK // P
UNIT = 5
UNITS = BLOCKS // UNIT
WIDE = UNIT * CHUNK
RING = 4
A_TILES = BLOCKS * CHUNKS // UNIT
RESIDENT = 4
PIECES = ((0, 2), (2, 5))
UNSCALE = float(2 ** (127 - MAX_NEIGH))
BIG = 128.0
NORM_STEPS = 20
SUM_STEPS = UNITS * UNIT - 1
LAST_STEPS = 8


def adjacency_layers(
    nc, x_rows, x_cols, adj_rows, adj_cols, w_layer0, w_layer1, per_node, rows_rep, pars_rep, out
):
    w_spill = nc.dram_tensor("w_spill", [CHUNKS - RESIDENT, UNITS, P, WIDE], U8, kind="Internal").ap()

    ctx = ExitStack()
    with ctx:
        def sb(name, shape, dt):
            return ctx.enter_context(nc.sbuf_tensor(name, shape, dt))

        def sem(name):
            return ctx.enter_context(nc.semaphore(name))

        adj = sb("adj", [P, RING, WIDE], F32)
        halves = sb("halves", [P, 4, WIDE], BF16)
        w_bytes = sb("w_bytes", [P, RESIDENT * UNITS * WIDE], U8)
        stage = sb("stage", [P, 2, WIDE], U8)
        X = sb("X", [P, BLOCKS, D], F32)
        hi_mid = sb("hi_mid", [P, BLOCKS, 2 * D], BF16)
        low = sb("low", [P, BLOCKS, D], BF16)
        t = sb("t", [P, BLOCKS, D], F32)
        e_now = sb("e_now", [P, 2, D], F32)
        hT = sb("hT", [P, CHUNK], F32)
        norm = [sb(f"norm{i}", [P, PER_CHUNK, D], F32) for i in range(3)]
        sums = sb("sums", [P, 2, PER_CHUNK], F32)
        rstd = sb("rstd", [P, 2, PER_CHUNK], F32)
        ident = sb("ident", [P, P], F32)
        rank_w = sb("rank_w", [P, P], BF16)
        minus_ones = sb("minus_ones", [P, P], BF16)
        sum0 = sb("sum0", [P, CHUNK], BF16)
        nodes = sb("nodes", [P, BLOCKS], F32)
        reps = sb("reps", [P, 3, D], F32)
        pars = sb("pars", [P, 4], F32)
        par_prod = sb("par_prod", [P, 2], F32)
        w0 = sb("w0", [D, 2 * D], F32)
        w1 = sb("w1", [P, D], F32)
        eps = sb("eps", [P, 1], F32)
        xT = w_bytes[0:D, 0:4 * N].bitcast(F32)
        tT = w_bytes[:, 4 * N:4 * N + 2 * N].bitcast(F32)
        e_all = hi_mid[:, :, :].bitcast(F32)

        psum = ctx.enter_context(nc.psum_tensor("psum", [P, 8 * CHUNK], F32))

        def bank(b, n=1):
            return psum[:, b * CHUNK:(b + n) * CHUNK]

        H_BANK, TURN_BANK = 5, 6
        gamma, beta, bias = (reps[:, i, :].unsqueeze(1).to_broadcast([P, PER_CHUNK, D]) for i in range(3))

        inputs_in = sem("inputs_in")
        adj_in = [sem(f"adj_in{s}") for s in range(RING)]
        consts_made = sem("consts_made")
        xw_made = sem("xw_made")
        pars_made = sem("pars_made")
        e_step = sem("e_step")
        e_staged = sem("e_staged")
        tiles_used = sem("tiles_used")
        tT_copied = sem("tT_copied")
        t_turned = sem("t_turned")
        t_made = sem("t_made")
        masks_made = sem("masks_made")
        sum_step = sem("sum_step")
        ranks_made = sem("ranks_made")
        ranks_out = sem("ranks_out")
        spilled = [sem(f"spilled{i}") for i in range(2)]
        hT_copied = sem("hT_copied")
        h_turned = sem("h_turned")
        norm_step = sem("norm_step")
        std_made = sem("std_made")
        bytes_in = [sem(f"bytes_in{s}") for s in range(RING)]
        w_by_dve = sem("w_by_dve")
        w_by_act = sem("w_by_act")
        w_used = sem("w_used")
        yT_copied = sem("yT_copied")
        o_made = sem("o_made")
        last_step = sem("last_step")
        last_std = sem("last_std")
        stored = sem("stored")
        block = ctx.enter_context(nc.Block())

        def block_of(g, b):
            return BLOCKS - 1 - (UNIT * g + b)

        def chunk_rows(j):
            return X[:, bass.ds(j * PER_CHUNK, PER_CHUNK), :]

        def resident_bytes(jc):
            return lambda k: w_bytes[:, (jc * UNITS + UNITS - 1 - k) * WIDE:(jc * UNITS + UNITS - k) * WIDE]

        def loaded_bytes(i):
            return lambda k: adj[:, 2 * i + k // 4, :].bitcast(U8)[:, (3 - k % 4) * WIDE:(4 - k % 4) * WIDE]

        def loaded_wait(pair, i):
            def waits(eng, k):
                if k % 4 < 2:
                    eng.wait_ge(bytes_in[2 * i + k // 4], 16 * (pair + 1))
            return waits

        @block.sync
        def _(sp):
            for dst, src in ((xT, x_cols), (w0[:, :], w_layer0), (X[:, :, :], x_rows), (nodes[:, :], per_node),
                             (reps[:, :, :], rows_rep), (pars[:, :], pars_rep), (w1[:, :], w_layer1)):
                sp.dma_start(dst, src).then_inc(inputs_in, 16)

            TILE = P * WIDE
            rows_flat = adj_rows.rearrange("n p c -> (n p c)")
            cols_flat = adj_cols.rearrange("j g p c -> (j g p c)")

            def load_tile(source, at, s):
                sp.dma_start(adj[:, s, :], source[bass.ds(at, TILE)].rearrange("(p c) -> p c", p=P))\
                    .then_inc(adj_in[s], 16)

            for s in range(RING):
                load_tile(rows_flat, s * TILE, s)
            with sp.Fori(1, A_TILES // RING) as turn:
                at = [sp.snap(turn * (RING * TILE) + s * TILE) for s in range(RING)]
                free = [sp.snap(RING * turn + (s - RING + 1)) for s in range(RING)]
                for s in range(RING):
                    sp.wait_ge(tiles_used, free[s])
                    load_tile(rows_flat, at[s], s)

            for g in range(RING):
                sp.wait_ge(tiles_used, A_TILES + g - RING + 1)
                load_tile(cols_flat, g * TILE, g)
            with sp.Fori(1, CHUNKS * UNITS // RING) as turn:
                at = [sp.snap(turn * (RING * TILE) + s * TILE) for s in range(RING)]
                free = [sp.snap(2 * RING * turn + 2 * (s - RING + 1)) for s in range(RING)]
                for s in range(RING):
                    sp.wait_ge(ranks_made, free[s])
                    load_tile(cols_flat, at[s], s)

            sp.wait_ge(ranks_made, 2 * CHUNKS * UNITS)
            for i in range(2):
                sp.wait_ge(spilled[i], 16 * (CHUNKS - RESIDENT) * UNITS // 2)

            for n in range(2 * (CHUNKS - RESIDENT)):
                s, g = n % RING, 4 - n % 2 * 4
                if n >= RING:
                    converted = (RESIDENT * UNITS + (n - RING + 1) * 4) // 2
                    sp.wait_ge(w_by_dve, converted)
                    sp.wait_ge(w_by_act, converted)
                sp.dma_start(adj[:, s, :].bitcast(U8).rearrange("p (g c) -> p g c", g=4),
                             w_spill[n // 2, g:g + 4, :, :].rearrange("g p c -> p g c")).then_inc(bytes_in[s], 16)

            parts = ((0, CHUNKS - 2), (CHUNKS - 2, CHUNKS))
            for a, b in parts:
                sp.wait_ge(last_step, LAST_STEPS * b)
                rows = slice(a * PER_CHUNK, b * PER_CHUNK)
                sp.dma_start(out[:, rows, :], X[:, rows, :]).then_inc(stored, 16)
            sp.wait_ge(stored, 16 * len(parts))

        @block.gpsimd
        def _(pool):
            nc.gpsimd.memset(ident[:, :], 0.0).then_inc(consts_made, 1)
            nc.gpsimd.memset(rank_w[:, :], -1.0).then_inc(consts_made, 1)
            nc.gpsimd.memset(minus_ones[:, :], -1.0).then_inc(consts_made, 1)
            nc.gpsimd.memset(sum0[:, :], 0.0).then_inc(consts_made, 1)
            nc.gpsimd.memset(eps[:, :], LN_EPS).then_inc(consts_made, 1)
            pool.wait_ge(consts_made, 5)
            nc.gpsimd.affine_select(out=ident[:, :], in_=ident[:, :], compare_op=ALU.not_equal, fill=1.0, base=0,
                                    pattern=[[-1, P]], channel_multiplier=1).then_inc(consts_made, 1)
            nc.gpsimd.affine_select(out=rank_w[:, :], in_=rank_w[:, :], compare_op=ALU.is_gt, fill=0.0, base=0,
                                    pattern=[[-1, P]], channel_multiplier=1).then_inc(consts_made, 1)
            nc.gpsimd.affine_select(out=sum0[:, :], in_=sum0[:, :], compare_op=ALU.not_equal, fill=BIG - MAX_NEIGH,
                                    base=0, pattern=[[0, CHUNK]], channel_multiplier=1).then_inc(consts_made, 1)
            pool.wait_ge(consts_made, 8)
            nc.gpsimd.affine_select(out=rank_w[:, :], in_=rank_w[:, :], compare_op=ALU.not_equal, fill=BIG, base=0,
                                    pattern=[[-1, P]], channel_multiplier=1).then_inc(consts_made, 1)
            pool.wait_ge(e_step, 12)
            for i in range(2):
                nc.gpsimd.tensor_copy(e_now[:, i, :], e_all[:, i, :]).then_inc(e_staged, 1)
            with pool.Fori(1, BLOCKS // 2) as pair:
                for i in range(2):
                    pool.wait_ge(tiles_used, 4 * pair + 2 * i - 2)
                    nc.gpsimd.tensor_copy(
                        e_now[:, i, :].unsqueeze(1), e_all[:, bass.ds(2 * pair + i, 1), :]
                    ).then_inc(e_staged, 1)

        @block.tensor
        def _(pe):
            pe.wait_ge(inputs_in, 16 * 7)
            pe.wait_ge(consts_made, 9)
            for k in range(BLOCKS // 8):
                for i in range(8):
                    b = 8 * k + i
                    w = w0[:, 0:D] if b < N_USERS // P else w0[:, D:2 * D]
                    last = nc.tensor.matmul(bank(k)[:, i * D:(i + 1) * D], xT[:, b * P:(b + 1) * P], w,
                                            start=True, stop=True)
                last.then_inc(xw_made, 1)

            def rows_times_e(pair, first, final):
                for i in range(2):
                    pe.wait_ge(e_staged, 2 * pair + i + 1)
                    for half in range(2):
                        s = 2 * i + half
                        pe.wait_ge(adj_in[s], 16 * (pair + 1))
                        for k in range(UNIT):
                            c = half * UNIT + k
                            low_row = c % 2 * D
                            last = nc.tensor.matmul(
                                bank(c // 2)[low_row:low_row + D, :], e_now[:, i, :], adj[:, s, k * CHUNK:(k + 1) * CHUNK],
                                start=first and i == 0, stop=final and i == 1)
                        last.then_inc(tiles_used, 1)

            rows_times_e(0, True, False)
            with pe.Fori(1, BLOCKS // 2 - 1) as pair:
                rows_times_e(pair, False, False)
            rows_times_e(BLOCKS // 2 - 1, False, True)

            for k in range(CHUNKS // 2):
                pe.wait_ge(tT_copied, k + 1)
                if k >= 3:
                    pe.wait_ge(t_made, 2 * (k - 2))
                for q in range(PER_CHUNK):
                    last = nc.tensor.transpose(bank(5 + k % 3)[:, q * P:(q + 1) * P],
                                               tT[:, k * CHUNK + q * P:k * CHUNK + (q + 1) * P], ident[:, :])
                last.then_inc(t_turned, 1)
            pe.wait_ge(t_made, CHUNKS)

            def turn_h(j, first):
                pe.wait_ge(hT_copied, j + 1)
                if not first:
                    pe.wait_ge(norm_step, (j - 1) * NORM_STEPS + 1)
                for q in range(PER_CHUNK):
                    last = nc.tensor.transpose(bank(TURN_BANK)[:, q * P:(q + 1) * P], hT[:, q * P:(q + 1) * P],
                                               ident[:, :])
                last.then_inc(h_turned, 1)

            def chunk_b(j, first, second=False):
                for g in range(UNITS):
                    v = j * UNITS + g
                    pe.wait_ge(adj_in[g % RING], 16 * (A_TILES // RING) + 16 * (2 * j + g // RING + 1))
                    if g == 0 and not first:
                        pe.wait_ge(hT_copied, j)
                    for b in range(UNIT):
                        row = (UNIT * g + b) % 2 * D
                        last = nc.tensor.matmul(
                            bank(H_BANK)[row:row + D, :], t[:, block_of(g, b), :],
                            adj[:, g % RING, b * CHUNK:(b + 1) * CHUNK],
                            start=g == 0 and b < 2, stop=g == UNITS - 1 and b >= UNIT - 2)
                    last.then_inc(tiles_used, 1)
                    if g == 1 and not first:
                        turn_h(j - 1, second)
                    pe.wait_ge(sum_step, j * SUM_STEPS + UNIT * (g + 1) - 1)
                    pe.wait_ge(masks_made, v + 1)
                    for n, (b0, b1) in enumerate(PIECES):
                        if not (first and g == 0):
                            pe.wait_ge(ranks_out, 2 * v + n - 1)
                        for b in range(b0, b1):
                            part = slice(b * CHUNK, (b + 1) * CHUNK)
                            nc.tensor.matmul(bank(b), rank_w[:, :], halves[:, g % 2, part], start=True, stop=False)
                            before = sum0[:, :] if g == 0 and b == 0 else halves[:, 2 + g % 2, part]
                            last = nc.tensor.matmul(bank(b), minus_ones[:, :], before, start=False, stop=True)
                        last.then_inc(ranks_made, 1)

            chunk_b(0, True)
            chunk_b(1, False, True)
            with pe.Fori(2, CHUNKS) as j:
                chunk_b(j, False)
            turn_h(CHUNKS - 1, False)

            def turn_y(jc, first):
                pe.wait_ge(yT_copied, jc + 1)
                if not first:
                    pe.wait_ge(last_step, LAST_STEPS * (jc - 1) + 1)
                for q in range(PER_CHUNK):
                    last = nc.tensor.matmul(bank(TURN_BANK)[:, q * D:(q + 1) * D], hT[:, q * P:(q + 1) * P], w1[:, :],
                                            start=True, stop=True)
                last.then_inc(o_made, 1)

            def chunk_c(jc, parity, place):
                for k in range(UNITS):
                    g = UNITS - 1 - k
                    if k == 0 and place >= 2:
                        pe.wait_ge(yT_copied, jc - 1)
                    ready = w_by_act if k % 2 else w_by_dve
                    pe.wait_ge(ready, jc * (UNITS // 2) + k // 2 + 1)
                    if g == 0:
                        pe.wait_ge(norm_step, CHUNKS * NORM_STEPS)
                    out_bank = bank(parity)
                    for b in range(UNIT):
                        nc.tensor.matmul(out_bank, hi_mid[:, block_of(g, b), :],
                                         halves[:, k % 4, b * CHUNK:(b + 1) * CHUNK],
                                         start=k == 0 and b == 0, stop=False, skip_group_check=True)
                    for b in range(UNIT):
                        row = (UNIT * k + b) % 2 * D
                        last = nc.tensor.matmul(out_bank[row:row + D, :], low[:, block_of(g, b), :],
                                                halves[:, k % 4, b * CHUNK:(b + 1) * CHUNK],
                                                start=False, stop=k == UNITS - 1 and b >= UNIT - 2,
                                                skip_group_check=True)
                    last.then_inc(w_used, 1)
                    if k == 1 and place >= 1:
                        turn_y(jc - 1, place == 1)

            pe.wait_ge(norm_step, (CHUNKS - 1) * NORM_STEPS)
            pe.wait_ge(ranks_out, 2 * CHUNKS * UNITS)
            for jc in range(RESIDENT):
                chunk_c(jc, jc % 2, jc)
            with pe.Fori(0, (CHUNKS - RESIDENT) // 2) as pair:
                for i in range(2):
                    chunk_c(2 * pair + (RESIDENT + i), i, RESIDENT)
            turn_y(CHUNKS - 1, False)

        @block.scalar
        def _(act):
            act.wait_ge(tiles_used, A_TILES)
            for k in range(CHUNKS // 2):
                nc.scalar.activation(tT[:, k * CHUNK:(k + 1) * CHUNK], bank(k), ACT.Copy).then_inc(tT_copied, 1)

            def std(n, steps, of_step, made):
                act.wait_ge(of_step, steps)
                nc.scalar.activation(rstd[:, n, :], sums[:, n, :], ACT.Sqrt, bias=eps[:, :], scale=1.0 / D)\
                    .then_inc(made, 1)

            def chunk_b(j, first, spill):
                for g in range(UNITS):
                    v = j * UNITS + g
                    if g == UNITS - 1:
                        act.wait_ge(tiles_used, A_TILES + (j + 1) * UNITS)
                        if not first:
                            act.wait_ge(h_turned, j)
                        nc.scalar.activation(hT[:, :], bank(H_BANK), ACT.Copy).then_inc(hT_copied, 1)
                    if spill:
                        to = stage[:, g % 2, :]
                        if not (spill == "first" and g < 2):
                            act.wait_ge(spilled[g % 2], 16 * ((j - RESIDENT) * (UNITS // 2) + g // 2))
                    else:
                        to = w_bytes[:, bass.ds(v * WIDE, WIDE)]
                    for n, (b0, b1) in enumerate(PIECES):
                        act.wait_ge(ranks_made, 2 * v + n + 1)
                        nc.scalar.activation(to[:, b0 * CHUNK:b1 * CHUNK], bank(b0, b1 - b0), ACT.Relu)\
                            .then_inc(ranks_out, 1)
                    if spill:
                        act.wait_ge(ranks_out, 2 * v + 2)
                        act.dma_start(w_spill[bass.ds(j - RESIDENT, 1), g, :, :].rearrange("a p c -> p (a c)"), to)\
                            .then_inc(spilled[g % 2], 16)
                    if not first and g == 2:
                        std(0, (j - 1) * NORM_STEPS + 5, norm_step, std_made)
                    if not first and g == 4:
                        std(1, (j - 1) * NORM_STEPS + 14, norm_step, std_made)

            chunk_b(0, True, None)
            with act.Fori(1, RESIDENT) as j:
                chunk_b(j, False, None)
            chunk_b(RESIDENT, False, "first")
            with act.Fori(RESIDENT + 1, CHUNKS) as j:
                chunk_b(j, False, "more")
            def copy_y(jc, parity, first):
                act.wait_ge(w_used, (jc + 1) * UNITS)
                if first:
                    act.wait_ge(h_turned, CHUNKS)
                else:
                    act.wait_ge(o_made, jc)
                nc.scalar.activation(hT[:, :], bank(parity), ACT.Copy).then_inc(yT_copied, 1)

            def convert(jc, parity, place, waits, source):
                for k in range(1, UNITS, 2):
                    waits(act, k)
                    if place == 0 and k < 4:
                        std(k // 2, (CHUNKS - 1) * NORM_STEPS + (5, 14)[k // 2], norm_step, std_made)
                        act.wait_ge(ranks_made, 2 * CHUNKS * UNITS)
                        act.wait_ge(sum_step, CHUNKS * SUM_STEPS)
                    else:
                        act.wait_ge(w_used, jc * UNITS + k - 3)
                    nc.scalar.activation(halves[:, k % 4, :].bitcast(U16), source(k), ACT.Copy, scale=128.0)\
                        .then_inc(w_by_act, 1)
                    if k == 1 and place >= 1:
                        copy_y(jc - 1, 1 - parity, place == 1)
                    if k == 5 and place >= 1:
                        std(0, LAST_STEPS * (jc - 1) + 6, last_step, last_std)

            act.wait_ge(ranks_out, 2 * CHUNKS * UNITS)
            for jc in range(RESIDENT):
                convert(jc, jc % 2, jc, lambda eng, k: None, resident_bytes(jc))
            with act.Fori(0, (CHUNKS - RESIDENT) // 2) as pair:
                for i in range(2):
                    convert(2 * pair + (RESIDENT + i), i, RESIDENT, loaded_wait(pair, i), loaded_bytes(i))
            copy_y(CHUNKS - 1, 1, False)
            std(0, LAST_STEPS * (CHUNKS - 1) + 6, last_step, last_std)

        @block.vector
        def _(dve):
            dve.wait_ge(inputs_in, 16 * 7)
            v4 = pars[:, :].rearrange("p (k two) -> p k two", two=2)
            nc.vector.tensor_tensor(par_prod[:, :], v4[:, :, 0], v4[:, :, 1], ALU.mult).then_inc(pars_made, 1)
            dve.wait_ge(pars_made, 1)
            users = N_USERS // P
            nc.vector.tensor_scalar(nodes[:, 0:users], nodes[:, 0:users], par_prod[:, 0:1], None, ALU.mult)\
                .then_inc(e_step, 1)
            nc.vector.tensor_scalar(nodes[:, users:BLOCKS], nodes[:, users:BLOCKS], par_prod[:, 1:2], None, ALU.mult)\
                .then_inc(e_step, 1)
            dve.wait_ge(e_step, 2)
            for k in range(BLOCKS // 8):
                dve.wait_ge(xw_made, k + 1)
                group = slice(8 * k, 8 * k + 8)
                nc.vector.tensor_tensor(
                    e_all[:, group, :], bank(k).rearrange("p (b d) -> p b d", d=D),
                    nodes[:, group].unsqueeze(2).to_broadcast([P, 8, D]), ALU.mult).then_inc(e_step, 1)
                dve.wait_ge(e_step, 2 * k + 3)
                nc.vector.tensor_tensor(e_all[:, group, :], e_all[:, group, :], X[:, group, :], ALU.add)\
                    .then_inc(e_step, 1)

            t_v = t[:, :, :].rearrange("p (c q) d -> p c q d", q=PER_CHUNK)
            for k in range(CHUNKS // 2):
                dve.wait_ge(t_turned, k + 1)
                turned = bank(5 + k % 3).rearrange("p (q h d) -> p q h d", q=PER_CHUNK, h=2)
                nc.vector.tensor_copy(t_v[:, 2 * k, :, :], turned[:, :, 0, :]).then_inc(t_made, 1)
                nc.vector.tensor_copy(t_v[:, 2 * k + 1, :, :], turned[:, :, 1, :]).then_inc(t_made, 1)

            a, b_, c_ = (n[:, :, :] for n in norm)

            def wide(v):
                return v.unsqueeze(2).to_broadcast([P, PER_CHUNK, D])

            def norm_part(j, part):
                base = j * NORM_STEPS
                done = [0, 5, 14, 20][part]

                def step(ins):
                    nonlocal done
                    ins.then_inc(norm_step, 1)
                    done += 1
                    dve.wait_ge(norm_step, base + done)

                if part == 0:
                    dve.wait_ge(h_turned, j + 1)
                    turned = bank(TURN_BANK).rearrange("p (q h d) -> p q h d", q=PER_CHUNK, h=2)
                    step(nc.vector.tensor_reduce(a, turned.rearrange("p q h d -> p q d h"), AX, ALU.add))
                    step(nc.vector.tensor_reduce(sums[:, 0, :], a, AX, ALU.add))
                    step(nc.vector.scalar_tensor_tensor(b_, wide(sums[:, 0, :]), -1.0 / D, a, ALU.mult, ALU.add))
                    step(nc.vector.tensor_tensor(a, b_, b_, ALU.mult))
                    step(nc.vector.tensor_reduce(sums[:, 0, :], a, AX, ALU.add))
                elif part == 1:
                    dve.wait_ge(std_made, 2 * j + 1)
                    step(nc.vector.reciprocal(rstd[:, 0, :], rstd[:, 0, :]))
                    step(nc.vector.tensor_tensor(a, b_, wide(rstd[:, 0, :]), ALU.mult))
                    step(nc.vector.tensor_tensor(a, a, gamma, ALU.mult))
                    step(nc.vector.tensor_tensor(a, a, beta, ALU.add))
                    step(nc.vector.scalar_tensor_tensor(a, chunk_rows(j), 2.0, a, ALU.mult, ALU.add))
                    step(nc.vector.tensor_reduce(sums[:, 1, :], a, AX, ALU.add))
                    step(nc.vector.scalar_tensor_tensor(b_, wide(sums[:, 1, :]), -1.0 / D, a, ALU.mult, ALU.add))
                    step(nc.vector.tensor_tensor(a, b_, b_, ALU.mult))
                    step(nc.vector.tensor_reduce(sums[:, 1, :], a, AX, ALU.add))
                else:
                    dve.wait_ge(std_made, 2 * j + 2)
                    blocks = bass.ds(j * PER_CHUNK, PER_CHUNK)
                    step(nc.vector.reciprocal(rstd[:, 1, :], rstd[:, 1, :]))
                    step(nc.vector.tensor_tensor(chunk_rows(j), b_, wide(rstd[:, 1, :]), ALU.mult))
                    step(nc.vector.tensor_scalar(hi_mid[:, blocks, 0:D], chunk_rows(j), UNSCALE, None, ALU.mult))
                    step(nc.vector.scalar_tensor_tensor(a, chunk_rows(j), UNSCALE, hi_mid[:, blocks, 0:D],
                                                        ALU.mult, ALU.subtract))
                    step(nc.vector.tensor_copy(hi_mid[:, blocks, D:2 * D], a))
                    step(nc.vector.tensor_tensor(low[:, blocks, :], a, hi_mid[:, blocks, D:2 * D], ALU.subtract))

            def chunk_b(j, first):
                for g in range(UNITS):
                    v = j * UNITS + g
                    dve.wait_ge(adj_in[g % RING], 16 * (A_TILES // RING) + 16 * (2 * j + g // RING + 1))
                    if not (first and g < 2):
                        dve.wait_ge(ranks_made, 2 * v - 2)
                    nc.vector.tensor_scalar(halves[:, g % 2, :], adj[:, g % RING, :], 0.0, None, ALU.not_equal)\
                        .then_inc(masks_made, 1)
                    for b in range(UNIT):
                        if g == 0 and b == 0:
                            continue
                        done = j * SUM_STEPS + UNIT * g + b - 1
                        if g == 0 and b == 1:
                            before, mask = sum0[:, :], halves[:, 0, 0:CHUNK]
                            if first:
                                dve.wait_ge(consts_made, 9)
                        elif b == 0:
                            before = halves[:, 2 + (g - 1) % 2, WIDE - CHUNK:WIDE]
                            mask = halves[:, (g - 1) % 2, WIDE - CHUNK:WIDE]
                            dve.wait_ge(sum_step, done)
                        else:
                            before = halves[:, 2 + g % 2, (b - 1) * CHUNK:b * CHUNK]
                            mask = halves[:, g % 2, (b - 1) * CHUNK:b * CHUNK]
                            dve.wait_ge(sum_step, done)
                        if b == 1:
                            dve.wait_ge(masks_made, v + 1)
                        nc.vector.tensor_tensor(halves[:, 2 + g % 2, b * CHUNK:(b + 1) * CHUNK], before, mask,
                                                ALU.add).then_inc(sum_step, 1)
                    if not first and g in (1, 3, 5):
                        norm_part(j - 1, g // 2)

            chunk_b(0, True)
            with dve.Fori(1, CHUNKS) as j:
                chunk_b(j, False)

            def last_norm(jc, part):
                done = [0, 6][part]

                def step(ins):
                    nonlocal done
                    ins.then_inc(last_step, 1)
                    done += 1
                    dve.wait_ge(last_step, LAST_STEPS * jc + done)

                if part == 0:
                    dve.wait_ge(o_made, jc + 1)
                    step(nc.vector.tensor_tensor(a, bank(TURN_BANK)[:, 0:PER_CHUNK * D].rearrange(
                        "p (q d) -> p q d", d=D), bias, ALU.add))
                    step(nc.vector.tensor_tensor(a, a, chunk_rows(jc), ALU.add))
                    step(nc.vector.tensor_reduce(sums[:, 0, :], a, AX, ALU.add))
                    step(nc.vector.scalar_tensor_tensor(b_, wide(sums[:, 0, :]), -1.0 / D, a, ALU.mult, ALU.add))
                    step(nc.vector.tensor_tensor(a, b_, b_, ALU.mult))
                    step(nc.vector.tensor_reduce(sums[:, 0, :], a, AX, ALU.add))
                else:
                    dve.wait_ge(last_std, jc + 1)
                    step(nc.vector.reciprocal(rstd[:, 0, :], rstd[:, 0, :]))
                    step(nc.vector.tensor_tensor(chunk_rows(jc), b_, wide(rstd[:, 0, :]), ALU.mult))

            def convert(jc, place, waits, source):
                for k in range(0, UNITS, 2):
                    waits(dve, k)
                    if place == 0 and k < 4:
                        norm_part(CHUNKS - 1, k // 2)
                        dve.wait_ge(ranks_made, 2 * CHUNKS * UNITS)
                        dve.wait_ge(ranks_out, 2 * CHUNKS * UNITS)
                    else:
                        dve.wait_ge(w_used, jc * UNITS + k - 3)
                    nc.vector.tensor_scalar(halves[:, k % 4, :].bitcast(U16), source(k), 128.0, None, ALU.mult)\
                        .then_inc(w_by_dve, 1)
                    if place == 0 and k == 2:
                        norm_part(CHUNKS - 1, 2)
                    if place >= 1 and k == 4:
                        last_norm(jc - 1, 0)
                    if place >= 1 and k == 6:
                        last_norm(jc - 1, 1)

            for jc in range(RESIDENT):
                convert(jc, jc, lambda eng, k: None, resident_bytes(jc))
            with dve.Fori(0, (CHUNKS - RESIDENT) // 2) as pair:
                for i in range(2):
                    convert(2 * pair + (RESIDENT + i), RESIDENT, loaded_wait(pair, i), loaded_bytes(i))
            last_norm(CHUNKS - 1, 0)
            last_norm(CHUNKS - 1, 1)


_INS = ["x_rows", "x_cols", "adj_rows", "adj_cols", "w_layer0", "w_layer1", "per_node", "rows_rep", "pars_rep"]


def kernel(x, adj, L0_gnn_W_u, L0_gnn_diag_u, L0_gnn_par_u, L0_gnn_W_i, L0_gnn_diag_i, L0_gnn_par_i,
           L0_gnn_ln_gamma, L0_gnn_ln_beta, L1_gnn_weight, L1_gnn_bias):
    import numpy as np
    import concourse.bacc as bacc
    from concourse.bass_utils import run_bass_kernel_spmd

    x, adj = np.asarray(x), np.asarray(adj)
    weight = np.asarray(L1_gnn_weight)
    rows = np.stack([np.asarray(v) for v in (L0_gnn_ln_gamma, L0_gnn_ln_beta, L1_gnn_bias)])
    pars = np.concatenate([np.asarray(L0_gnn_par_u), np.asarray(L0_gnn_par_i)])
    cols = adj.reshape(CHUNKS, CHUNK, BLOCKS, P)[:, :, ::-1, :].reshape(CHUNKS, CHUNK, UNITS, UNIT, P)
    arrays = {
        "x_rows": x.reshape(BLOCKS, P, D).transpose(1, 0, 2),
        "x_cols": x.T,
        "adj_rows": adj.reshape(BLOCKS, P, 2, WIDE).transpose(0, 2, 1, 3).reshape(A_TILES, P, WIDE),
        "adj_cols": cols.transpose(0, 2, 4, 3, 1).reshape(CHUNKS, UNITS, P, WIDE),
        "w_layer0": np.concatenate([np.asarray(L0_gnn_W_u), np.asarray(L0_gnn_W_i)], axis=1),
        "w_layer1": np.concatenate([weight, weight], axis=0),
        "per_node": np.concatenate([np.asarray(L0_gnn_diag_u), np.asarray(L0_gnn_diag_i)]).reshape(BLOCKS, P).T,
        "rows_rep": np.broadcast_to(rows, (P, 3, D)),
        "pars_rep": np.broadcast_to(pars, (P, 4)),
    }
    arrays = {name: np.ascontiguousarray(a) for name, a in arrays.items()}
    nc = bacc.Bacc("TRN2", target_bir_lowering=False, num_devices=1)
    args = [nc.dram_tensor(n, arrays[n].shape, F32, kind="ExternalInput").ap() for n in _INS]
    out = nc.dram_tensor("out_rows", (P, BLOCKS, D), F32, kind="ExternalOutput").ap()
    adjacency_layers(nc, *args, out)
    result = run_bass_kernel_spmd(nc, [arrays], core_ids=[0]).results[0]["out_rows"]
    return np.ascontiguousarray(result.reshape(P, BLOCKS, D).transpose(1, 0, 2)).reshape(N, D)
```

```python
from contextlib import ExitStack

import concourse.bass as bass
from concourse import mybir

F32 = mybir.dt.float32
BF16 = mybir.dt.bfloat16
U8 = mybir.dt.uint8
U16 = mybir.dt.uint16
ALU = mybir.AluOpType
ACT = mybir.ActivationFunctionType
AX = mybir.AxisListType.X

P = 128
N = 5120
D = 64
N_USERS = 2048
MAX_NEIGH = 100
LN_EPS = 1e-5
BLOCKS = N // P
CHUNK = 512
CHUNKS = N // CHUNK
PER_CHUNK = CHUNK // P
UNIT = 5
UNITS = BLOCKS // UNIT
WIDE = UNIT * CHUNK
RING = 4
A_TILES = BLOCKS * CHUNKS // UNIT
RESIDENT = 5
PAIRS = BLOCKS // 2
TURNED = 4
TURNS = WIDE // P // TURNED
HALF = CHUNK // 2
RANKS = 2 * UNIT
UNSCALE = float(2 ** (127 - MAX_NEIGH))
BIG = 128.0
SHIFT = BIG - MAX_NEIGH - 1
FULL = CHUNKS - RESIDENT
LEFT, RIGHT, BOTH = (0, HALF), (HALF, CHUNK), (0, CHUNK)
B_PRODUCTS = (((0, 0, LEFT), (1, 1, LEFT)), ((0, 0, RIGHT), (1, 1, RIGHT)), ((2, 0, LEFT), (3, 1, LEFT)),
              ((2, 0, RIGHT), (3, 1, RIGHT)), ((4, 0, LEFT), (4, 1, RIGHT)))
WIDE_PRODUCTS = ((0, 0, BOTH), (1, 1, BOTH), (2, 0, BOTH), (3, 1, BOTH), (4, 0, LEFT), (4, 1, RIGHT))
EARLY = UNITS // 2
LATE = [(0, 0), (0, 1), (0, 2), (1, 0), (1, 1), (1, 2), (0, 3), (1, 3)] + [
    (jc, g) for jc in range(2, RESIDENT) for g in range(EARLY)]
LATE_0 = RESIDENT * EARLY
COMPLETE = {jc: LATE_0 + max(n for n, (c, _) in enumerate(LATE) if c == jc) for jc in range(RESIDENT)}
TURN_Y_AFTER = {29: 0, 31: 1, 34: 2, 38: 3}
COPY_Y_AFTER = {29: 0, 31: 1, 35: 2, 39: 3}
LAST_STD_AFTER = {33: 0, 35: 1, 37: 2}
LAST_NORM_AFTER = {32: ((0, 0),), 34: ((0, 1), (1, 0)), 36: ((1, 1), (2, 0)), 38: ((2, 1),)}
E_STEPS0 = 2
CONSTS = 14
NORM_STEPS = 20
LAST_STEPS = 8


def adjacency_layers(
    nc, x_rows, x_cols, adj_rows, adj_cols, w_layer0, w_layer1, per_node, rows_rep, pars_rep, out
):
    w_spill = nc.dram_tensor("w_spill", [FULL, UNITS, P, WIDE // 4], F32, kind="Internal").ap()

    ctx = ExitStack()
    with ctx:
        def sb(name, shape, dt):
            return ctx.enter_context(nc.sbuf_tensor(name, shape, dt))

        def sem(name):
            return ctx.enter_context(nc.semaphore(name))

        adj = sb("adj", [P, RING, WIDE], F32)
        halves = sb("halves", [P, 4, WIDE], BF16)
        w_bytes = sb("w_bytes", [P, PAIRS * BLOCKS * P], U8)
        stage = sb("stage", [P, 2, WIDE], U8)
        X = sb("X", [P, BLOCKS, D], F32)
        hi_mid = sb("hi_mid", [P, BLOCKS, 2 * D], BF16)
        low = sb("low", [P, BLOCKS, D], BF16)
        t = sb("t", [P, BLOCKS, D], F32)
        e_now = sb("e_now", [P, 2, D], F32)
        hT = sb("hT", [P, CHUNK], F32)
        norm = [sb(f"norm{i}", [P, PER_CHUNK, D], F32) for i in range(2)]
        sums = sb("sums", [P, 2, PER_CHUNK], F32)
        rstd = sb("rstd", [P, 2, PER_CHUNK], F32)
        ident = sb("ident", [P, P], F32)
        rank_w = sb("rank_w", [P, P], BF16)
        rest_w = sb("rest_w", [P, P], BF16)
        minus_ident = sb("minus_ident", [P, P], BF16)
        big_ident = sb("big_ident", [P, P], BF16)
        shift = sb("shift", [P, 1], BF16)
        nodes = sb("nodes", [P, BLOCKS], F32)
        reps = sb("reps", [P, 3, D], F32)
        pars = sb("pars", [P, 4], F32)
        par_prod = sb("par_prod", [P, 2], F32)
        w1 = sb("w1", [P, D], F32)
        eps = sb("eps", [P, 1], F32)
        xT = w_bytes[0:D, 0:4 * N].bitcast(F32)
        w0 = t[0:D, 0:2, :].rearrange("p two d -> p (two d)")
        xwT = halves[:, 0:2, :].rearrange("p s c -> p (s c)").bitcast(F32)
        more_stage = hi_mid[:, 0:PAIRS, :].rearrange("p b d -> p (b d)").bitcast(U8)
        stages = [stage[:, 0, :], stage[:, 1, :], more_stage[:, 0:WIDE], more_stage[:, WIDE:2 * WIDE]]
        e_all = hi_mid[:, :, :].bitcast(F32)
        tT = hi_mid[:, :, :].rearrange("p b d -> p (b d)").bitcast(F32)

        psum = ctx.enter_context(nc.psum_tensor("psum", [P, 8 * CHUNK], F32))

        def bank(b, n=1):
            return psum[:, b * CHUNK:(b + n) * CHUNK]

        H_BANK, TURN_BANK = 5, 6
        T_BANKS = (5, 6, 7, 2, 3)

        def turn_bank(at):
            return 5 + (at % 3 if at < 2 * TURNS - 1 else 1)

        gamma, beta, bias = (reps[:, i, :].unsqueeze(1).to_broadcast([P, PER_CHUNK, D]) for i in range(3))

        xT_in = sem("xT_in")
        inputs_in = sem("inputs_in")
        small_in = sem("small_in")
        adj_in = [sem(f"adj_in{s}") for s in range(RING)]
        consts_made = sem("consts_made")
        xw_made = sem("xw_made")
        xwT_copied = sem("xwT_copied")
        xw_turned = sem("xw_turned")
        pars_made = sem("pars_made")
        e_step = sem("e_step")
        e_staged = sem("e_staged")
        tiles_used = sem("tiles_used")
        tT_copied = sem("tT_copied")
        t_turned = sem("t_turned")
        t_made = sem("t_made")
        row_masks = sem("row_masks")
        row_counts = sem("row_counts")
        rows_turned = sem("rows_turned")
        row_bytes = sem("row_bytes")
        masks_made = sem("masks_made")
        ranks_made = sem("ranks_made")
        ranks_out = sem("ranks_out")
        spilled = [sem(f"spilled{i}") for i in range(len(stages))]
        hT_copied = sem("hT_copied")
        h_turned = sem("h_turned")
        norm_step = sem("norm_step")
        std_made = sem("std_made")
        bytes_in = [sem(f"bytes_in{s}") for s in range(RING)]
        w_by_dve = sem("w_by_dve")
        w_by_act = sem("w_by_act")
        w_used = sem("w_used")
        yT_copied = sem("yT_copied")
        o_made = sem("o_made")
        last_step = sem("last_step")
        last_std = sem("last_std")
        stored = sem("stored")
        block = ctx.enter_context(nc.Block())

        def chunk_rows(j):
            return X[:, bass.ds(j * PER_CHUNK, PER_CHUNK), :]

        def unit_at(k):
            return (k + UNITS // 2) % UNITS

        bytes_v = w_bytes[:, :].rearrange("p (q r) -> p q r", q=PAIRS)

        def resident_bytes(jc, g):
            return bytes_v[:, bass.ds(PER_CHUNK * jc, PER_CHUNK), g * UNIT * P:(g + 1) * UNIT * P]

        def resident_weights(k):
            return halves[:, k % 4, :].bitcast(U16).rearrange("p (q r) -> p q r", q=PER_CHUNK)

        def loaded_bytes(i):
            return lambda k: adj[:, 2 * i + k // 4, :].bitcast(U8)[:, k % 4 * WIDE:(k % 4 + 1) * WIDE]

        def loaded_weights(k):
            return halves[:, k % 4, :].bitcast(U16)

        def weights_of(place, b, c0, c1, resident):
            if resident:
                return halves[:, place, :].rearrange("p (q b c) -> p q b c", q=PER_CHUNK, b=UNIT)[
                    :, c0 // P:c1 // P, b, :]
            return halves[:, place, b * CHUNK + c0:b * CHUNK + c1]

        def loaded_wait(pair, i):
            def waits(eng, k):
                if k % 4 < 2:
                    eng.wait_ge(bytes_in[2 * i + k // 4], 16 * (pair + 1))
            return waits

        @block.sync
        def _(sp):
            for dst, src in ((w0, w_layer0), (xT, x_cols)):
                sp.dma_start(dst, src).then_inc(xT_in, 16)
            for dst, src in ((nodes[:, :], per_node), (pars[:, :], pars_rep), (X[:, :, :], x_rows)):
                sp.dma_start(dst, src).then_inc(inputs_in, 16)

            TILE = P * WIDE
            rows_flat = adj_rows.rearrange("n p c -> (n p c)")
            cols_flat = adj_cols.rearrange("j g p c -> (j g p c)")

            def load_tile(source, at, s):
                sp.dma_start(adj[:, s, :], source[bass.ds(at, TILE)].rearrange("(p c) -> p c", p=P))\
                    .then_inc(adj_in[s], 16)

            for s in range(RING):
                load_tile(rows_flat, s * TILE, s)
            for dst, src in ((reps[:, :, :], rows_rep), (w1[:, :], w_layer1)):
                sp.dma_start(dst, src).then_inc(small_in, 16)
            with sp.Fori(1, A_TILES // RING) as turn:
                at = [sp.snap(turn * (RING * TILE) + s * TILE) for s in range(RING)]
                free = [sp.snap(RING * turn + (s - RING + 1)) for s in range(RING)]
                masked = [sp.snap(2 * turn + (s - 1)) for s in range(2)]
                for s in range(RING):
                    sp.wait_ge(tiles_used, free[s])
                    if s < 2:
                        sp.wait_ge(row_masks, masked[s])
                    load_tile(rows_flat, at[s], s)

            sp.wait_ge(row_masks, 2 * PAIRS)
            for g in range(RING):
                sp.wait_ge(tiles_used, A_TILES + g - RING + 1)
                load_tile(cols_flat, g * TILE, g)
            spill_flat = w_spill.rearrange("j g p c -> (j g p c)")

            def column_turn(turn, spill):
                at = [sp.snap(turn * (RING * TILE) + s * TILE) for s in range(RING)]
                free = [sp.snap(RING * turn + (A_TILES + s - RING + 1)) for s in range(RING)]
                if spill:
                    written = [sp.snap(turn * (RING * RANKS) + (s - RING + 1) * RANKS) for s in range(RING)]
                    to = [sp.snap((turn - 1) * (TILE // 4 * RING) + TILE // 4 * s) for s in range(RING)]
                for s in range(RING):
                    sp.wait_ge(tiles_used, free[s])
                    load_tile(cols_flat, at[s], s)
                    if spill:
                        sp.wait_ge(ranks_out, written[s])
                        sp.dma_start(spill_flat[bass.ds(to[s], TILE // 4)].rearrange("(p c) -> p c", p=P),
                                     stages[s].bitcast(F32))\
                            .then_inc(spilled[s], 16)

            with sp.Fori(1, FULL * UNITS // RING + 1) as turn:
                column_turn(turn, True)
            with sp.Fori(FULL * UNITS // RING + 1, CHUNKS * UNITS // RING) as turn:
                column_turn(turn, False)

            sp.wait_ge(tiles_used, A_TILES + CHUNKS * UNITS)
            for spill in spilled:
                sp.wait_ge(spill, 16 * FULL * UNITS // len(stages))

            for n in range(2 * (CHUNKS - RESIDENT)):
                s, g = n % RING, 4 - n % 2 * 4
                if n >= RING:
                    converted = (RESIDENT * UNITS + (n - RING + 1) * 4) // 2
                    sp.wait_ge(w_by_dve, converted)
                    sp.wait_ge(w_by_act, converted)
                sp.dma_start(adj[:, s, :].rearrange("p (g c) -> p g c", g=4),
                             w_spill[n // 2, g:g + 4, :, :].rearrange("g p c -> p g c")).then_inc(bytes_in[s], 16)

            parts = ((0, CHUNKS - 2), (CHUNKS - 2, CHUNKS))
            for a, b in parts:
                sp.wait_ge(last_step, LAST_STEPS * b)
                rows = slice(a * PER_CHUNK, b * PER_CHUNK)
                sp.dma_start(out[:, rows, :], X[:, rows, :]).then_inc(stored, 16)
            sp.wait_ge(stored, 16 * len(parts))

        @block.gpsimd
        def _(pool):
            for value, tile in ((0.0, ident), (-1.0, rank_w), (0.0, rest_w), (0.0, minus_ident), (0.0, big_ident),
                                (LN_EPS, eps), (SHIFT, shift)):
                nc.gpsimd.memset(tile[:, :], value).then_inc(consts_made, 1)
            pool.wait_ge(consts_made, 7)

            def select(tile, compare, fill):
                nc.gpsimd.affine_select(out=tile[:, :], in_=tile[:, :], compare_op=compare, fill=fill, base=0,
                                        pattern=[[1, P]], channel_multiplier=-1).then_inc(consts_made, 1)

            select(ident, ALU.not_equal, 1.0)
            select(minus_ident, ALU.not_equal, -1.0)
            select(big_ident, ALU.not_equal, BIG)
            select(rank_w, ALU.is_gt, 0.0)
            select(rest_w, ALU.is_ge, -1.0)
            pool.wait_ge(consts_made, 12)
            select(rank_w, ALU.not_equal, BIG - 1.0)
            select(rest_w, ALU.not_equal, -BIG)
            pool.wait_ge(e_step, E_STEPS0 + 3 * (PAIRS // (2 * PER_CHUNK) + 1))
            for i in range(2):
                nc.gpsimd.tensor_copy(e_now[:, i, :], e_all[:, PAIRS * i, :]).then_inc(e_staged, 1)
            pool.wait_ge(e_step, E_STEPS0 + 3 * (CHUNKS // 2))
            with pool.Fori(1, PAIRS) as pair:
                for i in range(2):
                    pool.wait_ge(tiles_used, 4 * pair + 2 * i - 2)
                    nc.gpsimd.tensor_copy(
                        e_now[:, i, :].unsqueeze(1), e_all[:, bass.ds(pair + PAIRS * i, 1), :]
                    ).then_inc(e_staged, 1)

        @block.tensor
        def _(pe):
            pe.wait_ge(xT_in, 16 * 2)
            pe.wait_ge(consts_made, CONSTS)
            for c in range(CHUNKS):
                w = w0[:, D:2 * D] if c < (N - N_USERS) // CHUNK else w0[:, 0:D]
                nc.tensor.matmul(bank(c // 2)[c % 2 * D:c % 2 * D + D, :], w, xT[:, c * CHUNK:(c + 1) * CHUNK],
                                 start=True, stop=True).then_inc(xw_made, 1)
            for k in range(CHUNKS // 2):
                pe.wait_ge(xwT_copied, k + 1)
                if k >= 3:
                    pe.wait_ge(e_step, E_STEPS0 + 3 * (k - 3) + 2)
                for q in range(PER_CHUNK):
                    at = k * CHUNK + q * P
                    last = nc.tensor.transpose(bank(5 + k % 3)[:, q * P:(q + 1) * P], xwT[:, at:at + P], ident[:, :])
                last.then_inc(xw_turned, 1)

            def tile_times_e(pair, s, first, final, turns, at_once=1):
                i, half = s // 2, s % 2
                if half == 0:
                    pe.wait_ge(e_staged, 2 * pair + i + 1)
                pe.wait_ge(adj_in[s], 16 * (pair + 1))
                for k in range(UNIT):
                    c = half * UNIT + k
                    low_row = c % 2 * D
                    last = nc.tensor.matmul(
                        bank(c // 2)[low_row:low_row + D, :], e_now[:, i, :], adj[:, s, k * CHUNK:(k + 1) * CHUNK],
                        start=first and i == 0, stop=final and i == 1, skip_group_check=True)
                    if k == UNIT - 1:
                        last.then_inc(tiles_used, 1)
                    if c % 2:
                        for turn in turns[:at_once]:
                            turn_rows(*turn)
                        del turns[:at_once]

            def turn_rows(pair, at, first=False):
                half, n = at // TURNS, at % TURNS
                if n == 0:
                    pe.wait_ge(row_counts, 2 * pair + half + 1)
                if not (first and at < 2):
                    pe.wait_ge(row_bytes, 2 * TURNS * pair + at - 1)
                for b in range(TURNED):
                    cols = slice((TURNED * n + b) * P, (TURNED * n + b + 1) * P)
                    to = bank(turn_bank(at))[:, b * P:(b + 1) * P]
                    nc.tensor.matmul(to, halves[:, 2 + half, cols], minus_ident[:, :], start=True, stop=False)
                    last = nc.tensor.matmul(to, halves[:, half, cols], big_ident[:, :], start=False, stop=True)
                last.then_inc(rows_turned, 1)

            def pair_a(pair, first, final):
                before = [] if first else [(pair - 1, TURNS + n) for n in range(TURNS)]
                tile_times_e(pair, 0, first, final, before)
                tile_times_e(pair, 1, first, final, before)
                turns = [(pair, n, first) for n in range(TURNS)]
                if final:
                    turns += [(pair, TURNS + n) for n in range(TURNS)]
                tile_times_e(pair, 2, first, final, turns, 2 if final else 1)
                tile_times_e(pair, 3, first, final, turns, 3 if final else 1)

            pair_a(0, True, False)
            with pe.Fori(1, PAIRS - 1) as pair:
                pair_a(pair, False, False)
            pair_a(PAIRS - 1, False, True)
            for k in range(CHUNKS // 2):
                pe.wait_ge(tT_copied, k + 1)
                if k == 0:
                    pe.wait_ge(row_bytes, 2 * TURNS * PAIRS)
                for q in range(PER_CHUNK):
                    last = nc.tensor.transpose(bank(T_BANKS[k])[:, q * P:(q + 1) * P],
                                               tT[:, k * CHUNK + q * P:k * CHUNK + (q + 1) * P], ident[:, :])
                last.then_inc(t_turned, 1)

            def turn_h(s, first):
                pe.wait_ge(hT_copied, s + 1)
                if not first:
                    pe.wait_ge(norm_step, (s - 1) * NORM_STEPS + 1)
                for q in range(PER_CHUNK):
                    last = nc.tensor.transpose(bank(TURN_BANK)[:, q * P:(q + 1) * P], hT[:, q * P:(q + 1) * P],
                                               ident[:, :])
                last.then_inc(h_turned, 1)

            def turn_y(jc, first=False):
                pe.wait_ge(yT_copied, jc + 1)
                if not first:
                    pe.wait_ge(last_step, LAST_STEPS * (jc - 1) + 1)
                for q in range(PER_CHUNK):
                    last = nc.tensor.matmul(bank(TURN_BANK)[:, q * D:(q + 1) * D], hT[:, q * P:(q + 1) * P], w1[:, :],
                                            start=True, stop=True)
                last.then_inc(o_made, 1)

            def weights_times_x(g, place, out_bank, first, final, resident):
                for b in range(UNIT):
                    nc.tensor.matmul(out_bank, hi_mid[:, UNIT * g + b, :], weights_of(place, b, 0, CHUNK, resident),
                                     start=first and b == 0, stop=False, skip_group_check=True)
                for b, upper, (c0, c1) in WIDE_PRODUCTS:
                    last = nc.tensor.matmul(out_bank[upper * D:(upper + 1) * D, c0:c1], low[:, UNIT * g + b, :],
                                            weights_of(place, b, c0, c1, resident),
                                            start=False, stop=final and b >= UNIT - 3, skip_group_check=True)
                last.then_inc(w_used, 1)

            def resident_unit(u, jc, g):
                pe.wait_ge(w_by_act if u % 2 else w_by_dve, u // 2 + 1)
                weights_times_x(g, u % 4, bank(jc), g == EARLY, u == COMPLETE[jc], True)

            def adj_times_t(g, products):
                for b, upper, (c0, c1) in products:
                    last = nc.tensor.matmul(
                        bank(H_BANK)[upper * D:(upper + 1) * D, c0:c1], t[:, UNIT * g + b, :],
                        adj[:, g % RING, b * CHUNK + c0:b * CHUNK + c1],
                        start=g == 0 and b < 2 and c0 == 0, stop=g == UNITS - 1 and b >= 2, skip_group_check=True)
                return last

            def chunk_b(s, ranks, first=False, second=False):
                for g in range(UNITS):
                    pe.wait_ge(adj_in[g % RING], 16 * (A_TILES // RING) + 16 * (2 * s + g // RING + 1))
                    if ranks:
                        pe.wait_ge(masks_made, s * UNITS + g + 1)
                    if g == 0 and not first:
                        pe.wait_ge(hT_copied, s)
                    if first:
                        pe.wait_ge(t_made, (UNIT * g + UNIT - 1) // PER_CHUNK + 1)
                    for b in range(UNIT if ranks else 0):
                        for half in range(2):
                            n = 2 * (UNIT * g + b) + half
                            if not (first and n < 2):
                                pe.wait_ge(ranks_out, s * RANKS * UNITS + n - 1)
                            to = bank(half)[:, 0:HALF]
                            if n < 2:
                                nc.tensor.matmul(to, minus_ident[:, :], shift[:, :].to_broadcast([P, HALF]),
                                                 start=True, stop=False, skip_group_check=True)
                            else:
                                g_, b_ = (g, b - 1) if b else (g - 1, UNIT - 1)
                                at = b_ * CHUNK + half * HALF
                                nc.tensor.matmul(to, rest_w[:, :], halves[:, g_ % RING, at:at + HALF],
                                                 start=False, stop=False, skip_group_check=True)
                            at = b * CHUNK + half * HALF
                            nc.tensor.matmul(to, rank_w[:, :], halves[:, g % RING, at:at + HALF], start=False,
                                             stop=True, skip_group_check=True).then_inc(ranks_made, 1)
                        last = adj_times_t(g, B_PRODUCTS[b])
                    if not ranks:
                        last = adj_times_t(g, WIDE_PRODUCTS)
                    last.then_inc(tiles_used, 1)
                    if g == 0 and not first:
                        turn_h(s - 1, second)
                    if not ranks and g % 2:
                        jc, n = s - FULL, g // 2
                        if s == FULL and g == 1:
                            pe.wait_ge(norm_step, (FULL - 1) * NORM_STEPS)
                            pe.wait_ge(ranks_out, FULL * RANKS * UNITS)
                        if s == FULL and n == EARLY - 1:
                            pe.wait_ge(norm_step, FULL * NORM_STEPS)
                        resident_unit(EARLY * jc + n, jc, EARLY + n)

            chunk_b(0, True, first=True)
            chunk_b(1, True, second=True)
            with pe.Fori(2, FULL) as s:
                chunk_b(s, True)
            for s in range(FULL, CHUNKS):
                chunk_b(s, False)
            turn_h(CHUNKS - 1, False)

            pe.wait_ge(small_in, 16 * 2)
            for n, (jc, g) in enumerate(LATE):
                u = LATE_0 + n
                if g == EARLY - 1:
                    pe.wait_ge(norm_step, CHUNKS * NORM_STEPS)
                resident_unit(u, jc, g)
                if u in TURN_Y_AFTER:
                    turn_y(TURN_Y_AFTER[u], first=u == min(TURN_Y_AFTER))

            def loaded_chunk(jc, parity):
                for k in range(UNITS):
                    if k == 0:
                        pe.wait_ge(yT_copied, jc - 1)
                    pe.wait_ge(w_by_act if k % 2 else w_by_dve, jc * (UNITS // 2) + k // 2 + 1)
                    weights_times_x(unit_at(k), k % 4, bank(parity), k == 0, k == UNITS - 1, False)
                    if k == 1:
                        turn_y(jc - 1)

            loaded_chunk(RESIDENT, RESIDENT % 2)
            with pe.Fori(0, (CHUNKS - RESIDENT - 1) // 2) as pair:
                for i in range(2):
                    loaded_chunk(2 * pair + (RESIDENT + 1 + i), i)
            turn_y(CHUNKS - 1)

        @block.scalar
        def _(act):
            nc.scalar.preload_act_table_set("sqrt_and_others")

            for k in range(CHUNKS // 2):
                act.wait_ge(xw_made, 2 * k + 2)
                nc.scalar.activation(xwT[:, k * CHUNK:(k + 1) * CHUNK], bank(k), ACT.Copy).then_inc(xwT_copied, 1)

            def write_row_bytes(pair, half):
                for n in range(TURNS):
                    at = half * TURNS + n
                    act.wait_ge(rows_turned, 2 * TURNS * pair + at + 1)
                    nc.scalar.activation(w_bytes[:, bass.ds(pair * (BLOCKS * P) + at * CHUNK, CHUNK)],
                                         bank(turn_bank(at)), ACT.Relu).then_inc(row_bytes, 1)

            write_row_bytes(0, 0)
            with act.Fori(1, PAIRS) as pair:
                write_row_bytes(pair - 1, 1)
                write_row_bytes(pair, 0)
            write_row_bytes(PAIRS - 1, 1)
            act.wait_ge(tiles_used, A_TILES)
            for k in range(CHUNKS // 2):
                nc.scalar.activation(tT[:, k * CHUNK:(k + 1) * CHUNK], bank(k), ACT.Copy).then_inc(tT_copied, 1)

            def std(n, steps, of_step, made):
                act.wait_ge(of_step, steps)
                nc.scalar.activation(rstd[:, n, :], sums[:, n, :], ACT.Sqrt, bias=eps[:, :], scale=1.0 / D)\
                    .then_inc(made, 1)

            def convert(u, to, source):
                if u is not None:
                    act.wait_ge(w_used, u - 3)
                nc.scalar.activation(to, source, ACT.Copy, scale=128.0).then_inc(w_by_act, 1)

            def copy_h(s, first=False):
                act.wait_ge(tiles_used, A_TILES + (s + 1) * UNITS)
                if not first:
                    act.wait_ge(h_turned, s)
                nc.scalar.activation(hT[:, :], bank(H_BANK), ACT.Copy).then_inc(hT_copied, 1)

            def chunk_b(s, ranks, first=False, early_0=False):
                for g in range(UNITS):
                    if not ranks and g in (0, 3):
                        jc, n = s - FULL, 1 if g == 0 else 3
                        convert(None if early_0 else EARLY * jc + n, resident_weights(n), resident_bytes(jc, EARLY + n))
                    if ranks:
                        place = g % len(stages)
                        if not (first and g < len(stages)):
                            act.wait_ge(spilled[place], 16 * (s * (UNITS // len(stages)) + g // len(stages)))
                        for n in range(RANKS):
                            at = s * RANKS * UNITS + g * RANKS + n
                            act.wait_ge(ranks_made, at + 1)
                            nc.scalar.activation(stages[place][:, n * HALF:(n + 1) * HALF], bank(n % 2)[:, 0:HALF],
                                                 ACT.Relu).then_inc(ranks_out, 1)
                    if not first and g == 2:
                        std(0, (s - 1) * NORM_STEPS + 5, norm_step, std_made)
                    if not first and g == 4:
                        std(1, (s - 1) * NORM_STEPS + 14, norm_step, std_made)

            act.wait_ge(t_turned, CHUNKS // 2)
            chunk_b(0, True, first=True)
            copy_h(0, first=True)
            with act.Fori(1, FULL) as s:
                chunk_b(s, True)
                copy_h(s)
            act.wait_ge(row_bytes, 2 * TURNS * PAIRS)
            act.wait_ge(ranks_made, FULL * RANKS * UNITS)
            chunk_b(FULL, False, early_0=True)
            copy_h(FULL)
            with act.Fori(FULL + 1, CHUNKS - 1) as s:
                chunk_b(s, False)
                copy_h(s)
            chunk_b(CHUNKS - 1, False)

            def copy_y(jc, used, of_bank):
                act.wait_ge(w_used, used)
                if isinstance(jc, int) and jc == 0:
                    act.wait_ge(h_turned, CHUNKS)
                else:
                    act.wait_ge(o_made, jc)
                nc.scalar.activation(hT[:, :], bank(of_bank), ACT.Copy).then_inc(yT_copied, 1)

            def last_std_of(jc):
                std(0, LAST_STEPS * jc + 6, last_step, last_std)

            def late(n):
                jc, g = LATE[n]
                convert(LATE_0 + n, resident_weights(n), resident_bytes(jc, g))

            late(1)
            copy_h(CHUNKS - 1)
            late(3)
            std(0, (CHUNKS - 1) * NORM_STEPS + 5, norm_step, std_made)
            late(5)
            std(1, (CHUNKS - 1) * NORM_STEPS + 14, norm_step, std_made)
            for n in range(7, len(LATE), 2):
                late(n)
                u = LATE_0 + n
                if u in COPY_Y_AFTER:
                    jc = COPY_Y_AFTER[u]
                    copy_y(jc, COMPLETE[jc] + 1, jc)
                if u in LAST_STD_AFTER:
                    last_std_of(LAST_STD_AFTER[u])

            def loaded_chunk(jc, bank_before, waits, source, first=False):
                for k in range(1, UNITS, 2):
                    waits(act, k)
                    convert(jc * UNITS + k, loaded_weights(k), source(k))
                    if k == 1:
                        if first:
                            last_std_of(RESIDENT - 2)
                        copy_y(jc - 1, jc * UNITS, bank_before)
                    if k == 5:
                        last_std_of(jc - 1)

            loaded_chunk(RESIDENT, RESIDENT - 1, loaded_wait(0, 0), loaded_bytes(0), first=True)
            with act.Fori(0, (CHUNKS - RESIDENT - 1) // 2) as pair:
                for i in range(2):
                    loaded_chunk(2 * pair + (RESIDENT + 1 + i), 1 - i, loaded_wait(pair + i, 1 - i), loaded_bytes(1 - i))
            copy_y(CHUNKS - 1, CHUNKS * UNITS, (CHUNKS - 1) % 2)
            last_std_of(CHUNKS - 1)

        @block.vector
        def _(dve):
            dve.wait_ge(inputs_in, 16 * 3)
            v4 = pars[:, :].rearrange("p (k two) -> p k two", two=2)
            nc.vector.tensor_tensor(par_prod[:, :], v4[:, :, 0], v4[:, :, 1], ALU.mult).then_inc(pars_made, 1)
            dve.wait_ge(pars_made, 1)
            items = (N - N_USERS) // P
            nc.vector.tensor_scalar(nodes[:, 0:items], nodes[:, 0:items], par_prod[:, 1:2], None, ALU.mult)\
                .then_inc(e_step, 1)
            nc.vector.tensor_scalar(nodes[:, items:BLOCKS], nodes[:, items:BLOCKS], par_prod[:, 0:1], None, ALU.mult)\
                .then_inc(e_step, 1)
            dve.wait_ge(e_step, E_STEPS0)
            for k in range(CHUNKS // 2):
                dve.wait_ge(xw_turned, k + 1)
                for half in range(2):
                    blocks = slice((2 * k + half) * PER_CHUNK, (2 * k + half + 1) * PER_CHUNK)
                    turned = bank(5 + k % 3).rearrange("p (q h d) -> p q h d", q=PER_CHUNK, h=2)[:, :, half, :]
                    nc.vector.tensor_tensor(e_all[:, blocks, :], turned, nodes[:, blocks].unsqueeze(2).to_broadcast(
                        [P, PER_CHUNK, D]), ALU.mult).then_inc(e_step, 1)
                dve.wait_ge(e_step, E_STEPS0 + 3 * k + 2)
                blocks = slice(2 * k * PER_CHUNK, (2 * k + 2) * PER_CHUNK)
                nc.vector.tensor_tensor(e_all[:, blocks, :], e_all[:, blocks, :], X[:, blocks, :], ALU.add)\
                    .then_inc(e_step, 1)

            def count_rows(pair, first):
                for half in range(2):
                    pe_done = 2 * TURNS * pair + (half - 1) * TURNS
                    dve.wait_ge(adj_in[half], 16 * (pair + 1))
                    if not first:
                        dve.wait_ge(rows_turned, pe_done)
                    nc.vector.tensor_scalar(halves[:, half, :], adj[:, half, :], 0.0, None, ALU.not_equal)\
                        .then_inc(row_masks, 1)
                    dve.wait_ge(row_masks, 2 * pair + half + 1)
                    if half:
                        dve.wait_ge(row_counts, 2 * pair + 1)
                    before = halves[:, 2, WIDE - 1:WIDE] if half else SHIFT
                    nc.vector.tensor_tensor_scan(halves[:, 2 + half, :], halves[:, half, :], halves[:, half, :],
                                                 before, ALU.add, ALU.max).then_inc(row_counts, 1)

            count_rows(0, True)
            with dve.Fori(1, PAIRS) as pair:
                count_rows(pair, False)

            a, b_ = (n[:, :, :] for n in norm)

            def wide(v):
                return v.unsqueeze(2).to_broadcast([P, PER_CHUNK, D])

            def norm_part(s, chunk, part):
                base = s * NORM_STEPS
                done = [0, 5, 14, 20][part]

                def step(ins):
                    nonlocal done
                    ins.then_inc(norm_step, 1)
                    done += 1
                    dve.wait_ge(norm_step, base + done)

                if part == 0:
                    dve.wait_ge(h_turned, s + 1)
                    turned = bank(TURN_BANK).rearrange("p (q h d) -> p q h d", q=PER_CHUNK, h=2)
                    step(nc.vector.tensor_reduce(a, turned.rearrange("p q h d -> p q d h"), AX, ALU.add))
                    step(nc.vector.tensor_reduce(sums[:, 0, :], a, AX, ALU.add))
                    step(nc.vector.scalar_tensor_tensor(b_, wide(sums[:, 0, :]), -1.0 / D, a, ALU.mult, ALU.add))
                    step(nc.vector.tensor_tensor(a, b_, b_, ALU.mult))
                    step(nc.vector.tensor_reduce(sums[:, 0, :], a, AX, ALU.add))
                elif part == 1:
                    dve.wait_ge(std_made, 2 * s + 1)
                    step(nc.vector.reciprocal(rstd[:, 0, :], rstd[:, 0, :]))
                    step(nc.vector.tensor_tensor(a, b_, wide(rstd[:, 0, :]), ALU.mult))
                    step(nc.vector.tensor_tensor(a, a, gamma, ALU.mult))
                    step(nc.vector.tensor_tensor(a, a, beta, ALU.add))
                    step(nc.vector.scalar_tensor_tensor(a, chunk_rows(chunk), 2.0, a, ALU.mult, ALU.add))
                    step(nc.vector.tensor_reduce(sums[:, 1, :], a, AX, ALU.add))
                    step(nc.vector.scalar_tensor_tensor(b_, wide(sums[:, 1, :]), -1.0 / D, a, ALU.mult, ALU.add))
                    step(nc.vector.tensor_tensor(a, b_, b_, ALU.mult))
                    step(nc.vector.tensor_reduce(sums[:, 1, :], a, AX, ALU.add))
                else:
                    dve.wait_ge(std_made, 2 * s + 2)
                    blocks = bass.ds(chunk * PER_CHUNK, PER_CHUNK)
                    step(nc.vector.reciprocal(rstd[:, 1, :], rstd[:, 1, :]))
                    step(nc.vector.tensor_tensor(chunk_rows(chunk), b_, wide(rstd[:, 1, :]), ALU.mult))
                    step(nc.vector.tensor_scalar(hi_mid[:, blocks, 0:D], chunk_rows(chunk), UNSCALE, None, ALU.mult))
                    step(nc.vector.scalar_tensor_tensor(a, chunk_rows(chunk), UNSCALE, hi_mid[:, blocks, 0:D],
                                                        ALU.mult, ALU.subtract))
                    step(nc.vector.tensor_copy(hi_mid[:, blocks, D:2 * D], a))
                    step(nc.vector.tensor_tensor(low[:, blocks, :], a, hi_mid[:, blocks, D:2 * D], ALU.subtract))

            def convert(u, to, source):
                if u is not None:
                    dve.wait_ge(w_used, u - 3)
                nc.vector.tensor_scalar(to, source, 128.0, None, ALU.mult).then_inc(w_by_dve, 1)

            def mask_columns(s, g):
                dve.wait_ge(adj_in[g % RING], 16 * (A_TILES // RING) + 16 * (2 * s + g // RING + 1))
                if not (isinstance(s, int) and g < RING):
                    dve.wait_ge(ranks_made, (s * UNITS + g - RING + 1) * RANKS + 2)
                nc.vector.tensor_scalar(halves[:, g % RING, :], adj[:, g % RING, :], 0.0, None,
                                        ALU.not_equal).then_inc(masks_made, 1)

            def chunk_b(s, ranks, chunk_before, first=False, early_0=False):
                for g in range(UNITS):
                    if not ranks and g in (0, 4):
                        jc = s - FULL
                        convert(None if early_0 else EARLY * jc + g // 2, resident_weights(g // 2),
                                resident_bytes(jc, EARLY + g // 2))
                    if ranks:
                        if not (first and g == 0):
                            mask_columns(s, g)
                    if not first and g in (2, 4, 6):
                        norm_part(s - 1, chunk_before, g // 2 - 1)

            dve.wait_ge(rows_turned, 2 * TURNS * PAIRS)
            mask_columns(0, 0)

            t_v = t[:, :, :].rearrange("p (c q) d -> p c q d", q=PER_CHUNK)
            for k in range(CHUNKS // 2):
                dve.wait_ge(t_turned, k + 1)
                turned = bank(T_BANKS[k]).rearrange("p (q h d) -> p q h d", q=PER_CHUNK, h=2)
                nc.vector.tensor_copy(t_v[:, 2 * k, :, :], turned[:, :, 0, :]).then_inc(t_made, 1)
                nc.vector.tensor_copy(t_v[:, 2 * k + 1, :, :], turned[:, :, 1, :]).then_inc(t_made, 1)

            dve.wait_ge(small_in, 16 * 2)
            chunk_b(0, True, None, first=True)
            with dve.Fori(1, FULL) as s:
                chunk_b(s, True, s + (RESIDENT - 1))
            dve.wait_ge(row_bytes, 2 * TURNS * PAIRS)
            dve.wait_ge(ranks_made, FULL * RANKS * UNITS)
            chunk_b(FULL, False, CHUNKS - 1, early_0=True)
            for spill in spilled:
                dve.wait_ge(spill, 16 * FULL * UNITS // len(stages))
            with dve.Fori(FULL + 1, CHUNKS) as s:
                chunk_b(s, False, s - (FULL + 1))

            def last_norm(jc, part):
                done = [0, 6][part]

                def step(ins):
                    nonlocal done
                    ins.then_inc(last_step, 1)
                    done += 1
                    dve.wait_ge(last_step, LAST_STEPS * jc + done)

                if part == 0:
                    dve.wait_ge(o_made, jc + 1)
                    step(nc.vector.tensor_tensor(a, bank(TURN_BANK)[:, 0:PER_CHUNK * D].rearrange(
                        "p (q d) -> p q d", d=D), bias, ALU.add))
                    step(nc.vector.tensor_tensor(a, a, chunk_rows(jc), ALU.add))
                    step(nc.vector.tensor_reduce(sums[:, 0, :], a, AX, ALU.add))
                    step(nc.vector.scalar_tensor_tensor(b_, wide(sums[:, 0, :]), -1.0 / D, a, ALU.mult, ALU.add))
                    step(nc.vector.tensor_tensor(a, b_, b_, ALU.mult))
                    step(nc.vector.tensor_reduce(sums[:, 0, :], a, AX, ALU.add))
                else:
                    dve.wait_ge(last_std, jc + 1)
                    step(nc.vector.reciprocal(rstd[:, 0, :], rstd[:, 0, :]))
                    step(nc.vector.tensor_tensor(chunk_rows(jc), b_, wide(rstd[:, 0, :]), ALU.mult))

            def late(n):
                jc, g = LATE[n]
                convert(LATE_0 + n, resident_weights(n), resident_bytes(jc, g))

            late(0)
            late(2)
            norm_part(CHUNKS - 1, RESIDENT - 1, 0)
            late(4)
            norm_part(CHUNKS - 1, RESIDENT - 1, 1)
            norm_part(CHUNKS - 1, RESIDENT - 1, 2)
            for n in range(6, len(LATE), 2):
                late(n)
                for jc, part in LAST_NORM_AFTER.get(LATE_0 + n, ()):
                    last_norm(jc, part)

            def loaded_chunk(jc, waits, source, first=False):
                for k in range(0, UNITS, 2):
                    waits(dve, k)
                    convert(jc * UNITS + k, loaded_weights(k), source(k))
                    if first and k < 4:
                        last_norm(RESIDENT - 2, k // 2)
                    if k >= 4:
                        last_norm(jc - 1, k // 2 - 2)

            loaded_chunk(RESIDENT, loaded_wait(0, 0), loaded_bytes(0), first=True)
            with dve.Fori(0, (CHUNKS - RESIDENT - 1) // 2) as pair:
                for i in range(2):
                    loaded_chunk(2 * pair + (RESIDENT + 1 + i), loaded_wait(pair + i, 1 - i), loaded_bytes(1 - i))
            last_norm(CHUNKS - 1, 0)
            last_norm(CHUNKS - 1, 1)


_INS = ["x_rows", "x_cols", "adj_rows", "adj_cols", "w_layer0", "w_layer1", "per_node", "rows_rep", "pars_rep"]


def kernel(x, adj, L0_gnn_W_u, L0_gnn_diag_u, L0_gnn_par_u, L0_gnn_W_i, L0_gnn_diag_i, L0_gnn_par_i,
           L0_gnn_ln_gamma, L0_gnn_ln_beta, L1_gnn_weight, L1_gnn_bias):
    import numpy as np
    import concourse.bacc as bacc
    from concourse.bass_utils import run_bass_kernel_spmd

    x, adj = np.asarray(x), np.asarray(adj)
    weight = np.asarray(L1_gnn_weight)
    x, adj = x[::-1], adj[::-1, ::-1]
    rows = np.stack([np.asarray(v) for v in (L0_gnn_ln_gamma, L0_gnn_ln_beta, L1_gnn_bias)])
    pars = np.concatenate([np.asarray(L0_gnn_par_u), np.asarray(L0_gnn_par_i)])
    by_rows = adj.reshape(2, PAIRS, P, 2, WIDE).transpose(1, 0, 3, 2, 4).reshape(A_TILES, P, WIDE)
    cols = adj.reshape(CHUNKS, CHUNK, UNITS, UNIT, P)
    cols = np.concatenate([cols[RESIDENT:], cols[:RESIDENT]])
    arrays = {
        "x_rows": x.reshape(BLOCKS, P, D).transpose(1, 0, 2),
        "x_cols": x.T,
        "adj_rows": by_rows,
        "adj_cols": cols.transpose(0, 2, 4, 3, 1).reshape(CHUNKS, UNITS, P, WIDE),
        "w_layer0": np.concatenate([np.asarray(L0_gnn_W_u), np.asarray(L0_gnn_W_i)], axis=1),
        "w_layer1": np.concatenate([weight, weight], axis=0),
        "per_node": np.concatenate([np.asarray(L0_gnn_diag_u), np.asarray(L0_gnn_diag_i)])[::-1].reshape(BLOCKS, P).T,
        "rows_rep": np.broadcast_to(rows, (P, 3, D)),
        "pars_rep": np.broadcast_to(pars, (P, 4)),
    }
    arrays = {name: np.ascontiguousarray(a) for name, a in arrays.items()}
    nc = bacc.Bacc("TRN2", target_bir_lowering=False, num_devices=1)
    args = [nc.dram_tensor(n, arrays[n].shape, F32, kind="ExternalInput").ap() for n in _INS]
    out = nc.dram_tensor("out_rows", (P, BLOCKS, D), F32, kind="ExternalOutput").ap()
    adjacency_layers(nc, *args, out)
    result = run_bass_kernel_spmd(nc, [arrays], core_ids=[0]).results[0]["out_rows"]
    return np.ascontiguousarray(result.reshape(P, BLOCKS, D).transpose(1, 0, 2).reshape(N, D)[::-1])
```

```python
from contextlib import ExitStack

import concourse.bass as bass
from concourse import mybir

F32 = mybir.dt.float32
BF16 = mybir.dt.bfloat16
U8 = mybir.dt.uint8
U16 = mybir.dt.uint16
ALU = mybir.AluOpType
ACT = mybir.ActivationFunctionType
AX = mybir.AxisListType.X

P = 128
N = 5120
D = 64
N_USERS = 2048
MAX_NEIGH = 100
LN_EPS = 1e-5
BLOCKS = N // P
CHUNK = 512
CHUNKS = N // CHUNK
PER_CHUNK = CHUNK // P
UNIT = 5
UNITS = BLOCKS // UNIT
WIDE = UNIT * CHUNK
RING = 4
A_TILES = BLOCKS * CHUNKS // UNIT
RESIDENT = 5
PAIRS = BLOCKS // 2
TURNED = 4
TURNS = WIDE // P // TURNED
HALF = CHUNK // 2
RANKS = 2 * UNIT
UNSCALE = float(2 ** (127 - MAX_NEIGH))
BIG = 128.0
SHIFT = BIG - MAX_NEIGH - 1
FULL = CHUNKS - RESIDENT
LEFT, RIGHT, BOTH = (0, HALF), (HALF, CHUNK), (0, CHUNK)
B_PRODUCTS = (((0, 0, LEFT), (1, 1, LEFT)), ((0, 0, RIGHT), (1, 1, RIGHT)), ((2, 0, LEFT), (3, 1, LEFT)),
              ((2, 0, RIGHT), (3, 1, RIGHT)), ((4, 0, LEFT), (4, 1, RIGHT)))
WIDE_PRODUCTS = ((0, 0, BOTH), (1, 1, BOTH), (2, 0, BOTH), (3, 1, BOTH), (4, 0, LEFT), (4, 1, RIGHT))
EARLY = (((0, 4), (0, 5), (0, 6), (1, 4), (1, 5), (1, 6)), ((0, 7), (1, 7), (2, 4), (2, 5), (2, 6), (2, 7)),
         ((3, 4), (3, 5), (3, 6), (3, 7), (4, 4), (4, 5)), ((4, 6), (4, 7), (0, 0), (1, 0), (2, 0), (3, 0)),
         ((4, 0), (0, 1), (1, 1), (2, 1), (3, 1), (4, 1)))
LATE = ((0, 2), (1, 2), (2, 2), (3, 2), (4, 2), (5, 4), (5, 5), (5, 6), (0, 3), (1, 3), (2, 3), (3, 3), (4, 3), (5, 7))
EARLY_BEFORE = (0, 1, 3, 4, 6, 7)
ORDER = [unit for chunk in EARLY for unit in chunk] + list(LATE)
LATE_0 = len(ORDER) - len(LATE)
ORDER += [unit for unit in ((jc, (k + UNITS // 2) % UNITS) for jc in range(RESIDENT, CHUNKS) for k in range(UNITS))
          if unit not in LATE]
ALL_UNITS = len(ORDER)


def early_before(s, g):
    return (s - FULL) * len(EARLY_BEFORE) + EARLY_BEFORE.index(g) if g in EARLY_BEFORE else None


def load_of(u):
    jc, g = ORDER[u]
    return None if jc < RESIDENT else 2 * (jc - RESIDENT) + (g < 4)


def last_of_load(n):
    return max(u for u in range(ALL_UNITS) if load_of(u) == n)


def complete(jc):
    return max(u for u, (c, _) in enumerate(ORDER) if c == jc)


def finish(jc):
    first = complete(jc) + 2
    if jc:
        first = max(first, finish(jc - 1) + 4)
    return first + 1 - first % 2


LAST_UNIT = finish(CHUNKS - 1) + 7
E_STEPS0 = 2
CONSTS = 14
NORM_STEPS = 20
LAST_STEPS = 8


def adjacency_layers(
    nc, x_rows, x_cols, adj_rows, adj_cols, w_layer0, w_layer1, per_node, rows_rep, pars_rep, out
):
    w_spill = nc.dram_tensor("w_spill", [FULL, UNITS, P, WIDE // 4], F32, kind="Internal").ap()

    ctx = ExitStack()
    with ctx:
        def sb(name, shape, dt):
            return ctx.enter_context(nc.sbuf_tensor(name, shape, dt))

        def sem(name):
            return ctx.enter_context(nc.semaphore(name))

        adj = sb("adj", [P, RING, WIDE], F32)
        halves = sb("halves", [P, 4, WIDE], BF16)
        w_bytes = sb("w_bytes", [P, PAIRS * BLOCKS * P], U8)
        stage = sb("stage", [P, 2, WIDE], U8)
        X = sb("X", [P, BLOCKS, D], F32)
        hi_mid = sb("hi_mid", [P, BLOCKS, 2 * D], BF16)
        low = sb("low", [P, BLOCKS, D], BF16)
        t = sb("t", [P, BLOCKS, D], F32)
        e_now = sb("e_now", [P, 2, D], F32)
        hT = sb("hT", [P, CHUNK], F32)
        norm = [sb(f"norm{i}", [P, PER_CHUNK, D], F32) for i in range(2)]
        sums = sb("sums", [P, 2, PER_CHUNK], F32)
        rstd = sb("rstd", [P, 2, PER_CHUNK], F32)
        ident = sb("ident", [P, P], F32)
        rank_w = sb("rank_w", [P, P], BF16)
        rest_w = sb("rest_w", [P, P], BF16)
        minus_ident = sb("minus_ident", [P, P], BF16)
        big_ident = sb("big_ident", [P, P], BF16)
        shift = sb("shift", [P, 1], BF16)
        nodes = sb("nodes", [P, BLOCKS], F32)
        reps = sb("reps", [P, 3, D], F32)
        pars = sb("pars", [P, 4], F32)
        par_prod = sb("par_prod", [P, 2], F32)
        w1 = sb("w1", [P, D], F32)
        eps = sb("eps", [P, 1], F32)
        xT = w_bytes[0:D, 0:4 * N].bitcast(F32)
        w0 = t[0:D, 0:2, :].rearrange("p two d -> p (two d)")
        xwT = halves[:, 0:2, :].rearrange("p s c -> p (s c)").bitcast(F32)
        more_stage = hi_mid[:, 0:PAIRS, :].rearrange("p b d -> p (b d)").bitcast(U8)
        stages = [stage[:, 0, :], stage[:, 1, :], more_stage[:, 0:WIDE], more_stage[:, WIDE:2 * WIDE]]
        e_all = hi_mid[:, :, :].bitcast(F32)
        tT = hi_mid[:, :, :].rearrange("p b d -> p (b d)").bitcast(F32)

        psum = ctx.enter_context(nc.psum_tensor("psum", [P, 8 * CHUNK], F32))

        def bank(b, n=1):
            return psum[:, b * CHUNK:(b + n) * CHUNK]

        H_BANK, TURN_BANK, Z_BANK = 5, 6, 7
        T_BANKS = (5, 6, 7, 2, 3)

        def turn_bank(at):
            return 5 + (at % 3 if at < 2 * TURNS - 1 else 1)

        gamma, beta, bias = (reps[:, i, :].unsqueeze(1).to_broadcast([P, PER_CHUNK, D]) for i in range(3))

        w0_in = sem("w0_in")
        xT_in = [sem(f"xT_in{i}") for i in range(2)]
        inputs_in = sem("inputs_in")
        small_in = sem("small_in")
        adj_in = [sem(f"adj_in{s}") for s in range(RING)]
        consts_made = sem("consts_made")
        xw_made = sem("xw_made")
        xwT_copied = sem("xwT_copied")
        xw_turned = sem("xw_turned")
        pars_made = sem("pars_made")
        e_step = sem("e_step")
        e_staged = sem("e_staged")
        tiles_used = sem("tiles_used")
        tT_copied = sem("tT_copied")
        t_turned = sem("t_turned")
        t_made = sem("t_made")
        row_masks = sem("row_masks")
        row_counts = sem("row_counts")
        rows_turned = sem("rows_turned")
        row_bytes = sem("row_bytes")
        masks_made = sem("masks_made")
        ranks_made = sem("ranks_made")
        ranks_out = sem("ranks_out")
        spilled = [sem(f"spilled{i}") for i in range(len(stages))]
        hT_copied = sem("hT_copied")
        h_turned = sem("h_turned")
        norm_step = sem("norm_step")
        std_made = sem("std_made")
        bytes_in = [sem(f"bytes_in{s}") for s in range(RING)]
        w_by_dve = sem("w_by_dve")
        w_by_act = sem("w_by_act")
        w_used = sem("w_used")
        yT_copied = sem("yT_copied")
        z_made = sem("z_made")
        zT_copied = sem("zT_copied")
        o_turned = sem("o_turned")
        last_step = sem("last_step")
        last_std = sem("last_std")
        stored = sem("stored")
        block = ctx.enter_context(nc.Block())

        def chunk_rows(j):
            return X[:, bass.ds(j * PER_CHUNK, PER_CHUNK), :]

        def out_bank_of(jc):
            return bank(jc if jc < RESIDENT else H_BANK if jc == RESIDENT else jc - RESIDENT - 1)

        def rows_ready(g):
            chunks = range(UNIT * g // PER_CHUNK, (UNIT * g + UNIT - 1) // PER_CHUNK + 1)
            return 1 + max((c - RESIDENT) % CHUNKS for c in chunks)

        bytes_v = w_bytes[:, :].rearrange("p (q r) -> p q r", q=PAIRS)

        def bytes_of(u):
            jc, g = ORDER[u]
            if jc < RESIDENT:
                return bytes_v[:, PER_CHUNK * jc:PER_CHUNK * (jc + 1), g * UNIT * P:(g + 1) * UNIT * P]
            return adj[:, load_of(u) % RING, :].bitcast(U8)[:, g % 4 * WIDE:(g % 4 + 1) * WIDE]

        def weights_to(u):
            to = halves[:, u % 4, :].bitcast(U16)
            return to.rearrange("p (q r) -> p q r", q=PER_CHUNK) if ORDER[u][0] < RESIDENT else to

        def bytes_wait(eng, u):
            n = load_of(u)
            if n is not None and n not in [load_of(v) for v in range(u % 2, u, 2)]:
                eng.wait_ge(bytes_in[n % RING], 16 * (n // RING + 1))

        def weights_of(place, b, c0, c1, resident):
            if resident:
                return halves[:, place, :].rearrange("p (q b c) -> p q b c", q=PER_CHUNK, b=UNIT)[
                    :, c0 // P:c1 // P, b, :]
            return halves[:, place, b * CHUNK + c0:b * CHUNK + c1]

        @block.sync
        def _(sp):
            sp.dma_start(w0, w_layer0).then_inc(w0_in, 16)
            for i in range(2):
                half = slice(i * N // 2, (i + 1) * N // 2)
                sp.dma_start(xT[:, half], x_cols[:, half]).then_inc(xT_in[i], 16)
            for dst, src in ((nodes[:, :], per_node), (pars[:, :], pars_rep), (X[:, :, :], x_rows)):
                sp.dma_start(dst, src).then_inc(inputs_in, 16)

            TILE = P * WIDE
            rows_flat = adj_rows.rearrange("n p c -> (n p c)")
            cols_flat = adj_cols.rearrange("j g p c -> (j g p c)")

            def load_tile(source, at, s):
                sp.dma_start(adj[:, s, :], source[bass.ds(at, TILE)].rearrange("(p c) -> p c", p=P))\
                    .then_inc(adj_in[s], 16)

            for s in range(RING):
                load_tile(rows_flat, s * TILE, s)
            for dst, src in ((reps[:, :, :], rows_rep), (w1[:, :], w_layer1)):
                sp.dma_start(dst, src).then_inc(small_in, 16)
            with sp.Fori(1, A_TILES // RING) as turn:
                at = [sp.snap(turn * (RING * TILE) + s * TILE) for s in range(RING)]
                free = [sp.snap(RING * turn + (s - RING + 1)) for s in range(RING)]
                masked = [sp.snap(2 * turn + (s - 1)) for s in range(2)]
                for s in range(RING):
                    sp.wait_ge(tiles_used, free[s])
                    if s < 2:
                        sp.wait_ge(row_masks, masked[s])
                    load_tile(rows_flat, at[s], s)

            sp.wait_ge(row_masks, 2 * PAIRS)
            for g in range(RING):
                sp.wait_ge(tiles_used, A_TILES + g - RING + 1)
                load_tile(cols_flat, g * TILE, g)
            spill_flat = w_spill.rearrange("j g p c -> (j g p c)")

            def column_turn(turn, spill):
                at = [sp.snap(turn * (RING * TILE) + s * TILE) for s in range(RING)]
                free = [sp.snap(RING * turn + (A_TILES + s - RING + 1)) for s in range(RING)]
                if spill:
                    written = [sp.snap(turn * (RING * RANKS) + (s - RING + 1) * RANKS) for s in range(RING)]
                    to = [sp.snap((turn - 1) * (TILE // 4 * RING) + TILE // 4 * s) for s in range(RING)]
                for s in range(RING):
                    sp.wait_ge(tiles_used, free[s])
                    load_tile(cols_flat, at[s], s)
                    if spill:
                        sp.wait_ge(ranks_out, written[s])
                        sp.dma_start(spill_flat[bass.ds(to[s], TILE // 4)].rearrange("(p c) -> p c", p=P),
                                     stages[s].bitcast(F32))\
                            .then_inc(spilled[s], 16)

            with sp.Fori(1, FULL * UNITS // RING + 1) as turn:
                column_turn(turn, True)
            with sp.Fori(FULL * UNITS // RING + 1, CHUNKS * UNITS // RING) as turn:
                column_turn(turn, False)

            sp.wait_ge(tiles_used, A_TILES + CHUNKS * UNITS)
            for spill in spilled:
                sp.wait_ge(spill, 16 * FULL * UNITS // len(stages))

            for n in range(2 * (CHUNKS - RESIDENT)):
                s, g = n % RING, 4 - n % 2 * 4
                if n >= RING:
                    converted = last_of_load(n - RING) + 1
                    sp.wait_ge(w_by_dve, (converted + 1) // 2)
                    sp.wait_ge(w_by_act, converted // 2)
                sp.dma_start(adj[:, s, :].rearrange("p (g c) -> p g c", g=4),
                             w_spill[n // 2, g:g + 4, :, :].rearrange("g p c -> p g c")).then_inc(bytes_in[s], 16)

            parts = ((0, CHUNKS - 1), (CHUNKS - 1, CHUNKS))
            for a, b in parts:
                sp.wait_ge(last_step, LAST_STEPS * b)
                rows = slice(a * PER_CHUNK, b * PER_CHUNK)
                sp.dma_start(out[:, rows, :], X[:, rows, :]).then_inc(stored, 16)
            sp.wait_ge(stored, 16 * len(parts))

        @block.gpsimd
        def _(pool):
            for value, tile in ((0.0, ident), (-1.0, rank_w), (0.0, rest_w), (0.0, minus_ident), (0.0, big_ident),
                                (LN_EPS, eps), (SHIFT, shift)):
                nc.gpsimd.memset(tile[:, :], value).then_inc(consts_made, 1)
            pool.wait_ge(consts_made, 7)

            def select(tile, compare, fill):
                nc.gpsimd.affine_select(out=tile[:, :], in_=tile[:, :], compare_op=compare, fill=fill, base=0,
                                        pattern=[[1, P]], channel_multiplier=-1).then_inc(consts_made, 1)

            select(ident, ALU.not_equal, 1.0)
            select(minus_ident, ALU.not_equal, -1.0)
            select(big_ident, ALU.not_equal, BIG)
            select(rank_w, ALU.is_gt, 0.0)
            select(rest_w, ALU.is_ge, -1.0)
            pool.wait_ge(consts_made, 12)
            select(rank_w, ALU.not_equal, BIG - 1.0)
            select(rest_w, ALU.not_equal, -BIG)
            pool.wait_ge(e_step, E_STEPS0 + 3 * (PAIRS // (2 * PER_CHUNK) + 1))
            for i in range(2):
                nc.gpsimd.tensor_copy(e_now[:, i, :], e_all[:, PAIRS * i, :]).then_inc(e_staged, 1)
            pool.wait_ge(e_step, E_STEPS0 + 3 * (CHUNKS // 2))
            with pool.Fori(1, PAIRS) as pair:
                for i in range(2):
                    pool.wait_ge(tiles_used, 4 * pair + 2 * i - 2)
                    nc.gpsimd.tensor_copy(
                        e_now[:, i, :].unsqueeze(1), e_all[:, bass.ds(pair + PAIRS * i, 1), :]
                    ).then_inc(e_staged, 1)

        @block.tensor
        def _(pe):
            pe.wait_ge(w0_in, 16)
            pe.wait_ge(consts_made, CONSTS)
            def turn_xw(k):
                pe.wait_ge(xwT_copied, k + 1)
                if k >= 3:
                    pe.wait_ge(e_step, E_STEPS0 + 3 * (k - 3) + 2)
                for q in range(PER_CHUNK):
                    at = k * CHUNK + q * P
                    last = nc.tensor.transpose(bank(5 + k % 3)[:, q * P:(q + 1) * P], xwT[:, at:at + P], ident[:, :])
                last.then_inc(xw_turned, 1)

            for c in range(CHUNKS):
                if c % (CHUNKS // 2) == 0:
                    pe.wait_ge(xT_in[c // (CHUNKS // 2)], 16)
                w = w0[:, D:2 * D] if c < (N - N_USERS) // CHUNK else w0[:, 0:D]
                nc.tensor.matmul(bank(c // 2)[c % 2 * D:c % 2 * D + D, :], w, xT[:, c * CHUNK:(c + 1) * CHUNK],
                                 start=True, stop=True).then_inc(xw_made, 1)
                if c % 2 and c > 1:
                    turn_xw(c // 2 - 1)
            turn_xw(CHUNKS // 2 - 1)

            def tile_times_e(pair, s, first, final, turns, at_once=1):
                i, half = s // 2, s % 2
                if half == 0:
                    pe.wait_ge(e_staged, 2 * pair + i + 1)
                pe.wait_ge(adj_in[s], 16 * (pair + 1))
                for k in range(UNIT):
                    c = half * UNIT + k
                    low_row = c % 2 * D
                    last = nc.tensor.matmul(
                        bank(c // 2)[low_row:low_row + D, :], e_now[:, i, :], adj[:, s, k * CHUNK:(k + 1) * CHUNK],
                        start=first and i == 0, stop=final and i == 1, skip_group_check=True)
                    if k == UNIT - 1:
                        last.then_inc(tiles_used, 1)
                    if c % 2:
                        for turn in turns[:at_once]:
                            turn_rows(*turn)
                        del turns[:at_once]

            def turn_rows(pair, at, first=False):
                half, n = at // TURNS, at % TURNS
                if n == 0:
                    pe.wait_ge(row_counts, 2 * pair + half + 1)
                if not (first and at < 2):
                    pe.wait_ge(row_bytes, 2 * TURNS * pair + at - 1)
                for b in range(TURNED):
                    cols = slice((TURNED * n + b) * P, (TURNED * n + b + 1) * P)
                    to = bank(turn_bank(at))[:, b * P:(b + 1) * P]
                    nc.tensor.matmul(to, halves[:, 2 + half, cols], minus_ident[:, :], start=True, stop=False)
                    last = nc.tensor.matmul(to, halves[:, half, cols], big_ident[:, :], start=False, stop=True)
                last.then_inc(rows_turned, 1)

            def pair_a(pair, first, final):
                before = [] if first else [(pair - 1, TURNS + n) for n in range(TURNS)]
                tile_times_e(pair, 0, first, final, before)
                tile_times_e(pair, 1, first, final, before)
                turns = [(pair, n, first) for n in range(TURNS)]
                if final:
                    turns += [(pair, TURNS + n) for n in range(TURNS)]
                tile_times_e(pair, 2, first, final, turns, 2 if final else 1)
                tile_times_e(pair, 3, first, final, turns, 3 if final else 1)

            pair_a(0, True, False)
            with pe.Fori(1, PAIRS - 1) as pair:
                pair_a(pair, False, False)
            pair_a(PAIRS - 1, False, True)

            for k in range(CHUNKS // 2):
                pe.wait_ge(tT_copied, k + 1)
                if k == 0:
                    pe.wait_ge(row_bytes, 2 * TURNS * PAIRS)
                for q in range(PER_CHUNK):
                    last = nc.tensor.transpose(bank(T_BANKS[k])[:, q * P:(q + 1) * P],
                                               tT[:, k * CHUNK + q * P:k * CHUNK + (q + 1) * P], ident[:, :])
                last.then_inc(t_turned, 1)

            def turn_h(s, first):
                pe.wait_ge(hT_copied, s + 1)
                if not first:
                    pe.wait_ge(norm_step, (s - 1) * NORM_STEPS + 1)
                for q in range(PER_CHUNK):
                    last = nc.tensor.transpose(bank(TURN_BANK)[:, q * P:(q + 1) * P], hT[:, q * P:(q + 1) * P],
                                               ident[:, :])
                last.then_inc(h_turned, 1)

            def y_times_weight(jc):
                pe.wait_ge(yT_copied, jc + 1)
                for upper, (c0, c1) in enumerate((LEFT, RIGHT)):
                    last = nc.tensor.matmul(bank(Z_BANK)[upper * D:(upper + 1) * D, 0:HALF], w1[:, :], hT[:, c0:c1],
                                            start=True, stop=True)
                last.then_inc(z_made, 1)

            def turn_z(jc):
                pe.wait_ge(zT_copied, jc + 1)
                if jc:
                    pe.wait_ge(last_step, LAST_STEPS * (jc - 1) + 1)
                for r in range(HALF // P):
                    last = nc.tensor.transpose(bank(TURN_BANK)[:, r * P:(r + 1) * P], hT[:, r * P:(r + 1) * P],
                                               ident[:, :])
                last.then_inc(o_turned, 1)

            def weights_times_x(g, place, out_bank, first, final, resident):
                for b in range(UNIT):
                    nc.tensor.matmul(out_bank, hi_mid[:, UNIT * g + b, :], weights_of(place, b, 0, CHUNK, resident),
                                     start=first and b == 0, stop=False, skip_group_check=True)
                for b, upper, (c0, c1) in WIDE_PRODUCTS:
                    last = nc.tensor.matmul(out_bank[upper * D:(upper + 1) * D, c0:c1], low[:, UNIT * g + b, :],
                                            weights_of(place, b, c0, c1, resident),
                                            start=False, stop=final and b >= UNIT - 3, skip_group_check=True)
                last.then_inc(w_used, 1)

            chunks_ready = FULL - 1

            def unit_c(u):
                nonlocal chunks_ready
                jc, g = ORDER[u]
                if rows_ready(g) > chunks_ready:
                    chunks_ready = rows_ready(g)
                    pe.wait_ge(norm_step, chunks_ready * NORM_STEPS)
                first = not any(c == jc for c, _ in ORDER[:u])
                if first and jc > RESIDENT:
                    pe.wait_ge(yT_copied, jc - RESIDENT)
                pe.wait_ge(w_by_act if u % 2 else w_by_dve, u // 2 + 1)
                weights_times_x(g, u % 4, out_bank_of(jc), first, u == complete(jc), jc < RESIDENT)

            def adj_times_t(g, products):
                for b, upper, (c0, c1) in products:
                    last = nc.tensor.matmul(
                        bank(H_BANK)[upper * D:(upper + 1) * D, c0:c1], t[:, UNIT * g + b, :],
                        adj[:, g % RING, b * CHUNK + c0:b * CHUNK + c1],
                        start=g == 0 and b < 2 and c0 == 0, stop=g == UNITS - 1 and b >= 2, skip_group_check=True)
                return last

            def chunk_b(s, ranks, first=False, second=False):
                for g in range(UNITS):
                    if not ranks and early_before(s, g) is not None:
                        if early_before(s, g) == 0:
                            pe.wait_ge(norm_step, (FULL - 1) * NORM_STEPS)
                            pe.wait_ge(ranks_out, FULL * RANKS * UNITS)
                        unit_c(early_before(s, g))
                    pe.wait_ge(adj_in[g % RING], 16 * (A_TILES // RING) + 16 * (2 * s + g // RING + 1))
                    if ranks:
                        pe.wait_ge(masks_made, s * UNITS + g + 1)
                    if first:
                        pe.wait_ge(t_made, (UNIT * g + UNIT - 1) // PER_CHUNK + 1)
                    for b in range(UNIT if ranks else 0):
                        for half in range(2):
                            n = 2 * (UNIT * g + b) + half
                            if not (first and n < 2):
                                pe.wait_ge(ranks_out, s * RANKS * UNITS + n - 1)
                            to = bank(half)[:, 0:HALF]
                            if n < 2:
                                nc.tensor.matmul(to, minus_ident[:, :], shift[:, :].to_broadcast([P, HALF]),
                                                 start=True, stop=False, skip_group_check=True)
                            else:
                                g_, b_ = (g, b - 1) if b else (g - 1, UNIT - 1)
                                at = b_ * CHUNK + half * HALF
                                nc.tensor.matmul(to, rest_w[:, :], halves[:, g_ % RING, at:at + HALF],
                                                 start=False, stop=False, skip_group_check=True)
                            at = b * CHUNK + half * HALF
                            nc.tensor.matmul(to, rank_w[:, :], halves[:, g % RING, at:at + HALF], start=False,
                                             stop=True, skip_group_check=True).then_inc(ranks_made, 1)
                        if g == 0 and b == 0 and not first:
                            pe.wait_ge(hT_copied, s)
                        last = adj_times_t(g, B_PRODUCTS[b])
                    if not ranks:
                        if g == 0:
                            pe.wait_ge(hT_copied, s)
                        last = adj_times_t(g, WIDE_PRODUCTS)
                    last.then_inc(tiles_used, 1)
                    if g == 0 and not first:
                        turn_h(s - 1, second)

            chunk_b(0, True, first=True)
            chunk_b(1, True, second=True)
            with pe.Fori(2, FULL) as s:
                chunk_b(s, True)
            for s in range(FULL, CHUNKS):
                chunk_b(s, False)

            pe.wait_ge(small_in, 16 * 2)
            for u in range(LATE_0, LAST_UNIT + 1):
                if u < ALL_UNITS:
                    unit_c(u)
                if u == LATE_0:
                    turn_h(CHUNKS - 1, False)
                for jc in range(CHUNKS):
                    if u == finish(jc):
                        y_times_weight(jc)
                    if u == finish(jc) + 2:
                        turn_z(jc)

        @block.scalar
        def _(act):
            nc.scalar.preload_act_table_set("sqrt_and_others")

            for k in range(CHUNKS // 2):
                act.wait_ge(xw_made, 2 * k + 2)
                nc.scalar.activation(xwT[:, k * CHUNK:(k + 1) * CHUNK], bank(k), ACT.Copy).then_inc(xwT_copied, 1)

            def write_row_bytes(pair, half):
                for n in range(TURNS):
                    at = half * TURNS + n
                    act.wait_ge(rows_turned, 2 * TURNS * pair + at + 1)
                    nc.scalar.activation(w_bytes[:, bass.ds(pair * (BLOCKS * P) + at * CHUNK, CHUNK)],
                                         bank(turn_bank(at)), ACT.Relu).then_inc(row_bytes, 1)

            write_row_bytes(0, 0)
            with act.Fori(1, PAIRS) as pair:
                write_row_bytes(pair - 1, 1)
                write_row_bytes(pair, 0)
            write_row_bytes(PAIRS - 1, 1)
            act.wait_ge(tiles_used, A_TILES)
            for k in range(CHUNKS // 2):
                nc.scalar.activation(tT[:, k * CHUNK:(k + 1) * CHUNK], bank(k), ACT.Copy).then_inc(tT_copied, 1)

            def std(n, steps, of_step, made):
                act.wait_ge(of_step, steps)
                nc.scalar.activation(rstd[:, n, :], sums[:, n, :], ACT.Sqrt, bias=eps[:, :], scale=1.0 / D)\
                    .then_inc(made, 1)

            def convert(u):
                bytes_wait(act, u)
                if u >= RING:
                    act.wait_ge(w_used, u - RING + 1)
                else:
                    act.wait_ge(ranks_made, min((FULL * UNITS - RING + u + 1) * RANKS + 2, FULL * UNITS * RANKS))
                nc.scalar.activation(weights_to(u), bytes_of(u), ACT.Copy, scale=128.0).then_inc(w_by_act, 1)

            def copy_h(s, first=False):
                act.wait_ge(tiles_used, A_TILES + (s + 1) * UNITS)
                if not first:
                    act.wait_ge(h_turned, s)
                nc.scalar.activation(hT[:, :], bank(H_BANK), ACT.Copy).then_inc(hT_copied, 1)

            def chunk_b(s, ranks, first=False):
                for g in range(UNITS):
                    if not ranks:
                        places = [(s, g + 1) if g < UNITS - 1 else (s + 1, 0)]
                        if s == FULL and g == 0:
                            places.insert(0, (s, 0))
                        for place in places:
                            u = early_before(*place) if place[0] < CHUNKS else None
                            if u is not None and u % 2:
                                convert(u)
                    if ranks:
                        place = g % len(stages)
                        if not (first and g < len(stages)):
                            act.wait_ge(spilled[place], 16 * (s * (UNITS // len(stages)) + g // len(stages)))
                        for n in range(RANKS):
                            at = s * RANKS * UNITS + g * RANKS + n
                            act.wait_ge(ranks_made, at + 1)
                            nc.scalar.activation(stages[place][:, n * HALF:(n + 1) * HALF], bank(n % 2)[:, 0:HALF],
                                                 ACT.Relu).then_inc(ranks_out, 1)
                    if not first and g == 2:
                        std(0, (s - 1) * NORM_STEPS + 5, norm_step, std_made)
                    if not first and g == 4:
                        std(1, (s - 1) * NORM_STEPS + 14, norm_step, std_made)

            act.wait_ge(t_turned, CHUNKS // 2)
            chunk_b(0, True, first=True)
            copy_h(0, first=True)
            with act.Fori(1, FULL) as s:
                chunk_b(s, True)
                copy_h(s)
            act.wait_ge(row_bytes, 2 * TURNS * PAIRS)
            for s in range(FULL, CHUNKS - 1):
                chunk_b(s, False)
                copy_h(s)
            chunk_b(CHUNKS - 1, False)

            late = [u for u in range(LATE_0, ALL_UNITS) if u % 2]
            convert(late[0])
            copy_h(CHUNKS - 1)
            convert(late[1])
            std(0, (CHUNKS - 1) * NORM_STEPS + 5, norm_step, std_made)
            convert(late[2])
            std(1, (CHUNKS - 1) * NORM_STEPS + 14, norm_step, std_made)
            for u in range(late[3], LAST_UNIT + 1, 2):
                if u < ALL_UNITS:
                    convert(u)
                for jc in range(CHUNKS):
                    if u == finish(jc):
                        act.wait_ge(w_used, complete(jc) + 1)
                        if jc:
                            act.wait_ge(o_turned, jc)
                        else:
                            act.wait_ge(h_turned, CHUNKS)
                        nc.scalar.activation(hT[:, :], out_bank_of(jc), ACT.Copy).then_inc(yT_copied, 1)
                    if u == finish(jc) + 2:
                        act.wait_ge(z_made, jc + 1)
                        nc.scalar.activation(hT[:, 0:HALF], bank(Z_BANK)[:, 0:HALF], ACT.Copy).then_inc(zT_copied, 1)
                    if u == finish(jc) + 6:
                        std(0, LAST_STEPS * jc + 6, last_step, last_std)

        @block.vector
        def _(dve):
            dve.wait_ge(inputs_in, 16 * 3)
            v4 = pars[:, :].rearrange("p (k two) -> p k two", two=2)
            nc.vector.tensor_tensor(par_prod[:, :], v4[:, :, 0], v4[:, :, 1], ALU.mult).then_inc(pars_made, 1)
            dve.wait_ge(pars_made, 1)
            items = (N - N_USERS) // P
            nc.vector.tensor_scalar(nodes[:, 0:items], nodes[:, 0:items], par_prod[:, 1:2], None, ALU.mult)\
                .then_inc(e_step, 1)
            nc.vector.tensor_scalar(nodes[:, items:BLOCKS], nodes[:, items:BLOCKS], par_prod[:, 0:1], None, ALU.mult)\
                .then_inc(e_step, 1)
            dve.wait_ge(e_step, E_STEPS0)
            for k in range(CHUNKS // 2):
                dve.wait_ge(xw_turned, k + 1)
                for half in range(2):
                    blocks = slice((2 * k + half) * PER_CHUNK, (2 * k + half + 1) * PER_CHUNK)
                    turned = bank(5 + k % 3).rearrange("p (q h d) -> p q h d", q=PER_CHUNK, h=2)[:, :, half, :]
                    nc.vector.tensor_tensor(e_all[:, blocks, :], turned, nodes[:, blocks].unsqueeze(2).to_broadcast(
                        [P, PER_CHUNK, D]), ALU.mult).then_inc(e_step, 1)
                dve.wait_ge(e_step, E_STEPS0 + 3 * k + 2)
                blocks = slice(2 * k * PER_CHUNK, (2 * k + 2) * PER_CHUNK)
                nc.vector.tensor_tensor(e_all[:, blocks, :], e_all[:, blocks, :], X[:, blocks, :], ALU.add)\
                    .then_inc(e_step, 1)

            def count_rows(pair, first):
                for half in range(2):
                    pe_done = 2 * TURNS * pair + (half - 1) * TURNS
                    dve.wait_ge(adj_in[half], 16 * (pair + 1))
                    if not first:
                        dve.wait_ge(rows_turned, pe_done)
                    nc.vector.tensor_scalar(halves[:, half, :], adj[:, half, :], 0.0, None, ALU.not_equal)\
                        .then_inc(row_masks, 1)
                    dve.wait_ge(row_masks, 2 * pair + half + 1)
                    if half:
                        dve.wait_ge(row_counts, 2 * pair + 1)
                    before = halves[:, 2, WIDE - 1:WIDE] if half else SHIFT
                    nc.vector.tensor_tensor_scan(halves[:, 2 + half, :], halves[:, half, :], halves[:, half, :],
                                                 before, ALU.add, ALU.max).then_inc(row_counts, 1)

            count_rows(0, True)
            with dve.Fori(1, PAIRS) as pair:
                count_rows(pair, False)

            a, b_ = (n[:, :, :] for n in norm)

            def wide(v):
                return v.unsqueeze(2).to_broadcast([P, PER_CHUNK, D])

            def norm_part(s, chunk, part):
                base = s * NORM_STEPS
                done = [0, 5, 14, 20][part]

                def step(ins):
                    nonlocal done
                    ins.then_inc(norm_step, 1)
                    done += 1
                    dve.wait_ge(norm_step, base + done)

                if part == 0:
                    dve.wait_ge(h_turned, s + 1)
                    turned = bank(TURN_BANK).rearrange("p (q h d) -> p q h d", q=PER_CHUNK, h=2)
                    step(nc.vector.tensor_reduce(a, turned.rearrange("p q h d -> p q d h"), AX, ALU.add))
                    step(nc.vector.tensor_reduce(sums[:, 0, :], a, AX, ALU.add))
                    step(nc.vector.scalar_tensor_tensor(b_, wide(sums[:, 0, :]), -1.0 / D, a, ALU.mult, ALU.add))
                    step(nc.vector.tensor_tensor(a, b_, b_, ALU.mult))
                    step(nc.vector.tensor_reduce(sums[:, 0, :], a, AX, ALU.add))
                elif part == 1:
                    dve.wait_ge(std_made, 2 * s + 1)
                    step(nc.vector.reciprocal(rstd[:, 0, :], rstd[:, 0, :]))
                    step(nc.vector.tensor_tensor(a, b_, wide(rstd[:, 0, :]), ALU.mult))
                    step(nc.vector.tensor_tensor(a, a, gamma, ALU.mult))
                    step(nc.vector.tensor_tensor(a, a, beta, ALU.add))
                    step(nc.vector.scalar_tensor_tensor(a, chunk_rows(chunk), 2.0, a, ALU.mult, ALU.add))
                    step(nc.vector.tensor_reduce(sums[:, 1, :], a, AX, ALU.add))
                    step(nc.vector.scalar_tensor_tensor(b_, wide(sums[:, 1, :]), -1.0 / D, a, ALU.mult, ALU.add))
                    step(nc.vector.tensor_tensor(a, b_, b_, ALU.mult))
                    step(nc.vector.tensor_reduce(sums[:, 1, :], a, AX, ALU.add))
                else:
                    dve.wait_ge(std_made, 2 * s + 2)
                    blocks = bass.ds(chunk * PER_CHUNK, PER_CHUNK)
                    step(nc.vector.reciprocal(rstd[:, 1, :], rstd[:, 1, :]))
                    step(nc.vector.tensor_tensor(chunk_rows(chunk), b_, wide(rstd[:, 1, :]), ALU.mult))
                    step(nc.vector.tensor_scalar(hi_mid[:, blocks, 0:D], chunk_rows(chunk), UNSCALE, None, ALU.mult))
                    step(nc.vector.scalar_tensor_tensor(a, chunk_rows(chunk), UNSCALE, hi_mid[:, blocks, 0:D],
                                                        ALU.mult, ALU.subtract))
                    step(nc.vector.tensor_copy(hi_mid[:, blocks, D:2 * D], a))
                    step(nc.vector.tensor_tensor(low[:, blocks, :], a, hi_mid[:, blocks, D:2 * D], ALU.subtract))

            def convert(u):
                bytes_wait(dve, u)
                if u >= RING:
                    dve.wait_ge(w_used, u - RING + 1)
                else:
                    dve.wait_ge(ranks_made, min((FULL * UNITS - RING + u + 1) * RANKS + 2, FULL * UNITS * RANKS))
                nc.vector.tensor_scalar(weights_to(u), bytes_of(u), 128.0, None, ALU.mult).then_inc(w_by_dve, 1)

            def mask_columns(s, g):
                dve.wait_ge(adj_in[g % RING], 16 * (A_TILES // RING) + 16 * (2 * s + g // RING + 1))
                if not (isinstance(s, int) and g < RING):
                    dve.wait_ge(ranks_made, (s * UNITS + g - RING + 1) * RANKS + 2)
                nc.vector.tensor_scalar(halves[:, g % RING, :], adj[:, g % RING, :], 0.0, None,
                                        ALU.not_equal).then_inc(masks_made, 1)

            def chunk_b(s, ranks, chunk_before, first=False):
                for g in range(UNITS):
                    if not ranks:
                        places = [(s, g + 1) if g < UNITS - 1 else (s + 1, 0)]
                        if s == FULL and g == 0:
                            places.insert(0, (s, 0))
                        for place in places:
                            u = early_before(*place) if place[0] < CHUNKS else None
                            if u is not None and u % 2 == 0:
                                convert(u)
                    if ranks:
                        if not (first and g == 0):
                            mask_columns(s, g)
                    if not first and g in (2, 4, 6):
                        norm_part(s - 1, chunk_before, g // 2 - 1)

            dve.wait_ge(rows_turned, 2 * TURNS * PAIRS)
            mask_columns(0, 0)

            t_v = t[:, :, :].rearrange("p (c q) d -> p c q d", q=PER_CHUNK)
            for k in range(CHUNKS // 2):
                dve.wait_ge(t_turned, k + 1)
                turned = bank(T_BANKS[k]).rearrange("p (q h d) -> p q h d", q=PER_CHUNK, h=2)
                nc.vector.tensor_copy(t_v[:, 2 * k, :, :], turned[:, :, 0, :]).then_inc(t_made, 1)
                nc.vector.tensor_copy(t_v[:, 2 * k + 1, :, :], turned[:, :, 1, :]).then_inc(t_made, 1)

            dve.wait_ge(small_in, 16 * 2)
            chunk_b(0, True, None, first=True)
            with dve.Fori(1, FULL) as s:
                chunk_b(s, True, s + (RESIDENT - 1))
            dve.wait_ge(row_bytes, 2 * TURNS * PAIRS)
            chunk_b(FULL, False, CHUNKS - 1)
            for spill in spilled:
                dve.wait_ge(spill, 16 * FULL * UNITS // len(stages))
            for s in range(FULL + 1, CHUNKS):
                chunk_b(s, False, s - (FULL + 1))

            def last_norm(jc, part):
                done = [0, 6][part]

                def step(ins):
                    nonlocal done
                    ins.then_inc(last_step, 1)
                    done += 1
                    dve.wait_ge(last_step, LAST_STEPS * jc + done)

                if part == 0:
                    dve.wait_ge(o_turned, jc + 1)
                    by_half = "p (h r) d -> p h r d"
                    step(nc.vector.tensor_tensor(
                        a.rearrange(by_half, h=2), bank(TURN_BANK)[:, 0:PER_CHUNK * D].rearrange(
                            "p (r h d) -> p h r d", r=2, h=2), bias.rearrange(by_half, h=2), ALU.add))
                    step(nc.vector.tensor_tensor(a, a, chunk_rows(jc), ALU.add))
                    step(nc.vector.tensor_reduce(sums[:, 0, :], a, AX, ALU.add))
                    step(nc.vector.scalar_tensor_tensor(b_, wide(sums[:, 0, :]), -1.0 / D, a, ALU.mult, ALU.add))
                    step(nc.vector.tensor_tensor(a, b_, b_, ALU.mult))
                    step(nc.vector.tensor_reduce(sums[:, 0, :], a, AX, ALU.add))
                else:
                    dve.wait_ge(last_std, jc + 1)
                    step(nc.vector.reciprocal(rstd[:, 0, :], rstd[:, 0, :]))
                    step(nc.vector.tensor_tensor(chunk_rows(jc), b_, wide(rstd[:, 0, :]), ALU.mult))

            late = [u for u in range(LATE_0, ALL_UNITS) if u % 2 == 0]
            convert(late[0])
            convert(late[1])
            norm_part(CHUNKS - 1, RESIDENT - 1, 0)
            convert(late[2])
            norm_part(CHUNKS - 1, RESIDENT - 1, 1)
            convert(late[3])
            norm_part(CHUNKS - 1, RESIDENT - 1, 2)
            for u in range(late[4], LAST_UNIT + 1, 2):
                if u < ALL_UNITS:
                    convert(u)
                for jc in range(CHUNKS):
                    if u == finish(jc) + 5:
                        last_norm(jc, 0)
                    if u == finish(jc) + 7:
                        last_norm(jc, 1)


_INS = ["x_rows", "x_cols", "adj_rows", "adj_cols", "w_layer0", "w_layer1", "per_node", "rows_rep", "pars_rep"]


def kernel(x, adj, L0_gnn_W_u, L0_gnn_diag_u, L0_gnn_par_u, L0_gnn_W_i, L0_gnn_diag_i, L0_gnn_par_i,
           L0_gnn_ln_gamma, L0_gnn_ln_beta, L1_gnn_weight, L1_gnn_bias):
    import numpy as np
    import concourse.bacc as bacc
    from concourse.bass_utils import run_bass_kernel_spmd

    x, adj = np.asarray(x), np.asarray(adj)
    weight = np.asarray(L1_gnn_weight)
    x, adj = x[::-1], adj[::-1, ::-1]
    rows = np.stack([np.asarray(v) for v in (L0_gnn_ln_gamma, L0_gnn_ln_beta, L1_gnn_bias)])
    pars = np.concatenate([np.asarray(L0_gnn_par_u), np.asarray(L0_gnn_par_i)])
    by_rows = adj.reshape(2, PAIRS, P, 2, WIDE).transpose(1, 0, 3, 2, 4).reshape(A_TILES, P, WIDE)
    cols = adj.reshape(CHUNKS, CHUNK, UNITS, UNIT, P)
    cols = np.concatenate([cols[RESIDENT:], cols[:RESIDENT]])
    arrays = {
        "x_rows": x.reshape(BLOCKS, P, D).transpose(1, 0, 2),
        "x_cols": x.T,
        "adj_rows": by_rows,
        "adj_cols": cols.transpose(0, 2, 4, 3, 1).reshape(CHUNKS, UNITS, P, WIDE),
        "w_layer0": np.concatenate([np.asarray(L0_gnn_W_u), np.asarray(L0_gnn_W_i)], axis=1),
        "w_layer1": np.concatenate([weight, weight], axis=0),
        "per_node": np.concatenate([np.asarray(L0_gnn_diag_u), np.asarray(L0_gnn_diag_i)])[::-1].reshape(BLOCKS, P).T,
        "rows_rep": np.broadcast_to(rows, (P, 3, D)),
        "pars_rep": np.broadcast_to(pars, (P, 4)),
    }
    arrays = {name: np.ascontiguousarray(a) for name, a in arrays.items()}
    nc = bacc.Bacc("TRN2", target_bir_lowering=False, num_devices=1)
    args = [nc.dram_tensor(n, arrays[n].shape, F32, kind="ExternalInput").ap() for n in _INS]
    out = nc.dram_tensor("out_rows", (P, BLOCKS, D), F32, kind="ExternalOutput").ap()
    adjacency_layers(nc, *args, out)
    result = run_bass_kernel_spmd(nc, [arrays], core_ids=[0]).results[0]["out_rows"]
    return np.ascontiguousarray(result.reshape(P, BLOCKS, D).transpose(1, 0, 2).reshape(N, D)[::-1])
```
